# Optimizing a Trainium2 kernel written in Bass

```python
import numpy as np
import jax
import jax.numpy as jnp

def _softmax(x, axis=-1):
    return jax.nn.softmax(x, axis=axis)

def _gelu(x):
    return jax.nn.gelu(x, approximate=True)

def _silu(x):
    return jax.nn.silu(x)

def _sigmoid(x):
    return jax.nn.sigmoid(x)

def _layernorm(x, axis=-1, eps=1e-05):
    m = jnp.mean(x, axis=axis, keepdims=True)
    v = jnp.var(x, axis=axis, keepdims=True)
    return (x - m) / jnp.sqrt(v + eps)

def _scatter_add(tgt, idx, src, axis=0):
    return tgt.at[idx].add(src)

def _segment_sum(src, seg, n):
    return jax.ops.segment_sum(src, seg, n)
kernel_name = 'mk_perceiver_d1_seqx_r2_6fbb17'

def setup_inputs(seed: int=0):
    np.random.seed(seed)
    _w = jnp.asarray

    def _rec_inputs():
        import jax
        import jax.numpy as jnp
        _rk = jax.random.key(seed)
        x = -0.0002928 + 1 * jax.random.normal(jax.random.fold_in(_rk, 1), (4, 128, 512), jnp.float32)
        _lenS = 128 - jax.random.randint(jax.random.fold_in(_rk, 7), (4,), 0, max(1, 128 // 4) + 1, jnp.int32)
        _lenS2 = 2048 - jax.random.randint(jax.random.fold_in(_rk, 8), (4,), 0, max(1, 2048 // 4) + 1, jnp.int32)
        _ctx_1024P = jax.random.normal(jax.random.fold_in(_rk, 11), (4, 16, 512), jnp.float32)
        _ctx_1024c = jax.random.dirichlet(jax.random.fold_in(_rk, 511), 0.3 * jnp.ones((16,), jnp.float32), (4, 2048))
        _ctx_1024t = jnp.einsum('bsk,bkd->bsd', _ctx_1024c, _ctx_1024P)
        _ctx_1024t = _ctx_1024t * jax.lax.rsqrt(jnp.mean(jnp.square(_ctx_1024t)) + 1e-12) * 0.953939
        ctx_1024 = -1.39393e-06 + 0.999914 * (_ctx_1024t + 0.3 * jax.random.normal(jax.random.fold_in(_rk, 611), (4, 2048, 512), jnp.float32))
        return (x, ctx_1024)
    x, ctx_1024 = _rec_inputs()

    def _L0_xattn_setup():
        import jax, jax.numpy as jnp
        import numpy as np
        HEADS = 16
        key = jax.random.key(seed)
        k1, k2, k3, k4 = jax.random.split(key, 4)
        B, T, S, W = (2, 1024, 1024, 512)
        x = jax.random.normal(k1, (B, T, W), dtype=jnp.float32)
        cond_k = jax.random.normal(k2, (B, S, W), dtype=jnp.float32)
        cond_v = jax.random.normal(k3, (B, S, W), dtype=jnp.float32)
        w_proj = jax.random.normal(k4, (W, W), dtype=jnp.float32) * 0.02
        b_proj = jnp.zeros((W,), dtype=jnp.float32)
        return {'x': x, 'cond_k': cond_k, 'cond_v': cond_v, 'w_proj': w_proj, 'b_proj': b_proj}
    _L0_xattn_all = _L0_xattn_setup()
    _L0_xattn_in = {k: v for k, v in _L0_xattn_all.items() if k in ('w_proj', 'b_proj')}
    del _L0_xattn_all

    def _L0_attn_setup():
        import jax, jax.numpy as jnp
        import numpy as np
        EPS = 1e-08

        def _gated_scan(dt, ut):
            a = 1.0 - dt
            b = dt * ut

            def combine(c1, c2):
                a1, b1 = c1
                a2, b2 = c2
                return (a2 * a1, a2 * b1 + b2)
            _, h = jax.lax.associative_scan(combine, (a, b), axis=1)
            return h
        key = jax.random.key(seed)
        ks = jax.random.split(key, 6)
        B, L, D, S = (4, 4096, 512, 64)
        sc = lambda fan_in: 1.0 / np.sqrt(fan_in)
        return {'x': jax.random.normal(ks[0], (B, L, D), dtype=jnp.float32), 'norm_w': jnp.ones((D,), dtype=jnp.float32), 'W_in': jax.random.normal(ks[1], (D, 3 * S), dtype=jnp.float32) * sc(D), 'b_in': jnp.zeros((3 * S,), dtype=jnp.float32), 'W_x': jax.random.normal(ks[2], (S, S), dtype=jnp.float32) * sc(S), 'b_x': jnp.zeros((S,), dtype=jnp.float32), 'W_dt': jax.random.normal(ks[3], (S, S), dtype=jnp.float32) * sc(S), 'b_dt': jnp.zeros((S,), dtype=jnp.float32), 'W_out': jax.random.normal(ks[4], (S, D), dtype=jnp.float32) * sc(S), 'b_out': jnp.zeros((D,), dtype=jnp.float32)}
    _L0_attn_all = _L0_attn_setup()
    _L0_attn_in = {k: v for k, v in _L0_attn_all.items() if k in ('norm_w', 'W_in', 'b_in', 'W_x', 'b_x', 'W_dt', 'b_dt', 'W_out', 'b_out')}
    del _L0_attn_all

    def _L0_ffn_setup():
        import jax, jax.numpy as jnp
        import numpy as np
        DIM = 512
        INTER = 512
        N_EXPERTS = 8
        TOPK = 2
        N_SHARED = 2
        key = jax.random.key(seed)
        ks = jax.random.split(key, 10)
        s = 0.02
        return {'x': jax.random.normal(ks[0], (4, 1024, DIM), dtype=jnp.float32), 'gate_w': jax.random.normal(ks[1], (N_EXPERTS, DIM), dtype=jnp.float32) * s, 'gate_bias': jax.random.normal(ks[2], (N_EXPERTS,), dtype=jnp.float32) * s, 'w1': jax.random.normal(ks[3], (N_EXPERTS, INTER, DIM), dtype=jnp.float32) * s, 'w3': jax.random.normal(ks[4], (N_EXPERTS, INTER, DIM), dtype=jnp.float32) * s, 'w2': jax.random.normal(ks[5], (N_EXPERTS, DIM, INTER), dtype=jnp.float32) * s, 'sw1': jax.random.normal(ks[6], (N_SHARED * INTER, DIM), dtype=jnp.float32) * s, 'sw3': jax.random.normal(ks[7], (N_SHARED * INTER, DIM), dtype=jnp.float32) * s, 'sw2': jax.random.normal(ks[8], (DIM, N_SHARED * INTER), dtype=jnp.float32) * s}
    _L0_ffn_all = _L0_ffn_setup()
    _L0_ffn_in = {k: v for k, v in _L0_ffn_all.items() if k in ('gate_w', 'gate_bias', 'w1', 'w3', 'w2', 'sw1', 'sw3', 'sw2')}
    del _L0_ffn_all
    return {'x': x, 'ctx_1024': ctx_1024, 'L0_xattn_w_proj': _L0_xattn_in['w_proj'], 'L0_xattn_b_proj': _L0_xattn_in['b_proj'], 'L0_attn_norm_w': _L0_attn_in['norm_w'], 'L0_attn_W_in': _L0_attn_in['W_in'], 'L0_attn_b_in': _L0_attn_in['b_in'], 'L0_attn_W_x': _L0_attn_in['W_x'], 'L0_attn_b_x': _L0_attn_in['b_x'], 'L0_attn_W_dt': _L0_attn_in['W_dt'], 'L0_attn_b_dt': _L0_attn_in['b_dt'], 'L0_attn_W_out': _L0_attn_in['W_out'], 'L0_attn_b_out': _L0_attn_in['b_out'], 'L0_ffn_gate_w': _L0_ffn_in['gate_w'], 'L0_ffn_gate_bias': _L0_ffn_in['gate_bias'], 'L0_ffn_w1': _L0_ffn_in['w1'], 'L0_ffn_w3': _L0_ffn_in['w3'], 'L0_ffn_w2': _L0_ffn_in['w2'], 'L0_ffn_sw1': _L0_ffn_in['sw1'], 'L0_ffn_sw3': _L0_ffn_in['sw3'], 'L0_ffn_sw2': _L0_ffn_in['sw2']}

def reference(x, ctx_1024, L0_xattn_w_proj, L0_xattn_b_proj, L0_attn_norm_w, L0_attn_W_in, L0_attn_b_in, L0_attn_W_x, L0_attn_b_x, L0_attn_W_dt, L0_attn_b_dt, L0_attn_W_out, L0_attn_b_out, L0_ffn_gate_w, L0_ffn_gate_bias, L0_ffn_w1, L0_ffn_w3, L0_ffn_w2, L0_ffn_sw1, L0_ffn_sw3, L0_ffn_sw2):
    import jax
    import jax.numpy as jnp

    def _L0_xattn_ref(x, cond_k, cond_v, w_proj, b_proj):
        import jax, jax.numpy as jnp
        import numpy as np
        HEADS = 16
        B, T, W = x.shape
        S = cond_k.shape[1]
        H = HEADS
        d = W // H
        scale = 1.0 / jnp.sqrt(jnp.sqrt(jnp.float32(d)))
        q = x.reshape(B, T, H, d) * scale
        k = cond_k.reshape(B, S, H, d) * scale
        v = cond_v.reshape(B, S, H, d)
        scores = jnp.einsum('bthd,bshd->bhts', q, k)
        w = jax.nn.softmax(scores.astype(jnp.float32), axis=-1).astype(scores.dtype)
        out = jnp.einsum('bhts,bshd->bthd', w, v).reshape(B, T, W)
        return out @ w_proj.T + b_proj

    def _L0_attn_ref(x, norm_w, W_in, b_in, W_x, b_x, W_dt, b_dt, W_out, b_out):
        import jax, jax.numpy as jnp
        import numpy as np
        EPS = 1e-08

        def _gated_scan(dt, ut):
            a = 1.0 - dt
            b = dt * ut

            def combine(c1, c2):
                a1, b1 = c1
                a2, b2 = c2
                return (a2 * a1, a2 * b1 + b2)
            _, h = jax.lax.associative_scan(combine, (a, b), axis=1)
            return h
        residual = x
        xn = x * jax.lax.rsqrt(jnp.mean(x * x, axis=-1, keepdims=True) + EPS) * norm_w
        p = jnp.einsum('bld,df->blf', xn, W_in) + b_in
        u, z, g = jnp.split(p, 3, axis=-1)
        ut = jnp.tanh(jnp.einsum('bls,st->blt', u, W_x) + b_x)
        dt = jax.nn.sigmoid(jnp.einsum('bls,st->blt', z, W_dt) + b_dt)
        h = _gated_scan(dt, ut)
        y = h * jax.nn.sigmoid(g)
        out = jnp.einsum('bls,sd->bld', y, W_out) + b_out
        return residual + out

    def _L0_ffn_ref(x, gate_w, gate_bias, w1, w3, w2, sw1, sw3, sw2):
        import jax, jax.numpy as jnp
        import numpy as np
        DIM = 512
        INTER = 512
        N_EXPERTS = 8
        TOPK = 2
        N_SHARED = 2
        shape = x.shape
        xt = x.reshape(-1, shape[-1])
        scores = jax.nn.softmax((xt @ gate_w.T).astype(jnp.float32), axis=-1)
        _, idx = jax.lax.top_k(scores + gate_bias, TOPK)
        weights = jnp.take_along_axis(scores, idx, axis=1).astype(x.dtype)
        y = jnp.zeros_like(xt)
        for e in range(N_EXPERTS):
            gate_e = jnp.sum(jnp.where(idx == e, weights, 0.0), axis=1)
            h = jax.nn.silu(xt @ w1[e].T) * (xt @ w3[e].T)
            y = y + gate_e[:, None] * (h @ w2[e].T)
        z = jax.nn.silu(xt @ sw1.T) * (xt @ sw3.T) @ sw2.T
        return (y + z).reshape(shape)
    x = x + _L0_xattn_ref(_layernorm(x, axis=-1), ctx_1024, ctx_1024, L0_xattn_w_proj, L0_xattn_b_proj)
    x = x + _L0_attn_ref(_layernorm(x, axis=-1), L0_attn_norm_w, L0_attn_W_in, L0_attn_b_in, L0_attn_W_x, L0_attn_b_x, L0_attn_W_dt, L0_attn_b_dt, L0_attn_W_out, L0_attn_b_out)
    x = x + _L0_ffn_ref(_layernorm(x, axis=-1), L0_ffn_gate_w, L0_ffn_gate_bias, L0_ffn_w1, L0_ffn_w3, L0_ffn_w2, L0_ffn_sw1, L0_ffn_sw3, L0_ffn_sw2)
    return x

_drawn_inputs = setup_inputs


def setup_inputs(seed=0):
    import zlib

    import numpy as np

    out = dict(_drawn_inputs(seed))
    spreads = {'L0_xattn_b_proj': (0.0, 0.1),
     'L0_attn_norm_w': (1.0, 0.588),
     'L0_attn_b_in': (0.0, 0.487),
     'L0_attn_b_x': (0.0, 0.486),
     'L0_attn_b_dt': (0.0, 0.8),
     'L0_attn_b_out': (0.0, 0.1)}
    factors = {'L0_ffn_gate_w': 8.0,
     'L0_ffn_gate_bias': 8.0,
     'L0_ffn_w1': 7.784,
     'L0_ffn_w3': 7.6,
     'L0_ffn_w2': 7.603,
     'L0_ffn_sw1': 8.0,
     'L0_ffn_sw3': 8.0,
     'L0_ffn_sw2': 8.0}
    for name, (base, spread) in spreads.items():
        noise = np.random.default_rng([zlib.crc32(name.encode()), seed]).standard_normal(out[name].shape)
        drawn = base * np.exp(spread * noise) if base else spread * noise
        out[name] = jnp.asarray(drawn.astype(out[name].dtype))
    for name, factor in factors.items():
        out[name] = (out[name] * factor).astype(out[name].dtype)
    return out
```

```python
import concourse.bass as bass
from concourse import mybir
import numpy as np

F32 = mybir.dt.float32
F16 = mybir.dt.float16
U32 = mybir.dt.uint32
ALU = mybir.AluOpType
ACT = mybir.ActivationFunctionType
AX = mybir.AxisListType

P = 128
B = 4
D = 512
C = D // P
S = 2048
J = S // P
HD = 32
HG = P // HD
G = B * C
T = B * P
ST = 64
E = 8
U = E + 2
HS = J // 2
MT = 2 + HG * HG
KS = 3 * HD
KM = KS + 2
SC = float(HD) ** -0.5
EPS = 1e-5
WS = 16.0


def build_program(nc, t, out):
    sb = nc.alloc_sbuf_tensor
    scoped = []

    def temp(name, shape, dt):
        h = nc.sbuf_tensor(name, shape, dt)
        scoped.append(h)
        return h.__enter__()

    x = sb("x_tok", [P, B, D], F32)
    xn = sb("xn", [P, B, D], F32)
    ao = sb("ao", [P, G, P], F32)
    wproj = sb("wproj", [P, C, D], F32)
    win = sb("win", [P, C, 3 * ST], F32)
    normw = sb("normw", [P, C], F32)
    bproj = sb("bproj", [P, D], F32)
    bout = sb("bout", [P, D], F32)
    wx = sb("wx", [P, ST], F32)
    wout = sb("wout", [ST, D], F32)
    cols = sb("cols", [P, 4], F32)
    gwt = sb("gwt", [P, C, E], F32)
    gbias = sb("gbias", [P, B, E], F32)
    iota = sb("iota", [P, E], F32)
    idf = sb("idf", [P, P], F32)
    idh = sb("idh", [P, P], F16)
    sel = sb("sel", [2 * U, U, P], F16)
    wst = sb("wst", [P, 2, 3, C, D], F32)
    zero = sb("zero", [P, 512], F16)
    mv = sb("mv", [P, B, 2], F32)
    st6 = sb("st6", [P, B, 6], F32)
    lnv = sb("lnv", [P, 8, B], F32)

    gwh = sb("gwh", [P, C, 2 * E], F16)
    lgs = sb("lgs", [P, 6, B, E], F32)
    top = sb("top", [P, B, 8], F32)
    topi = sb("topi", [P, B, 8], U32)
    topf = sb("topf", [P, B, 8], F32)
    r1 = sb("r1", [P, 3, B], F32)
    g20 = sb("g20", [P, B, 2 * U], F16)
    gT = sb("gT", [2 * U, T], F16)

    kt = temp("kt", [P, 2, S], F32)
    kh = temp("kh", [P, 2, S], F16)
    kl = temp("kl", [P, 2, S], F16)
    kstk = temp("kstk", [KM, 2, HG, S], F16)
    v = temp("v", [P, 2, J, P], F32)
    pt = temp("pt", [P, 4, 2, HG, P], F32)
    ps2 = temp("ps2", [P, 4, HG, P], F32)
    xs = temp("xs", [P, 2, HG, KM], F16)
    q1 = temp("q1", [KS, HG, P], F16)
    q2 = temp("q2", [KM, 2, HG, P], F16)
    mx = temp("mx", [P, HG, HG], F32)
    negm = temp("negm", [P, HG], F32)
    rden = temp("rden", [P, P], F32)
    ones = temp("ones", [P, HD], F32)
    for h in reversed(scoped):
        h.__exit__(None, None, None)
    scoped.clear()

    wh = temp("wh", [P, 2, 3, C, D], F16)
    wl = temp("wl", [P, 2, 3, C, D], F16)
    gate = temp("gate", [P, U, T], F32)
    xh = temp("xh", [P, C, T], F16)
    xl = temp("xl", [P, C, T], F16)
    sil = temp("sil", [P, 2, T], F32)
    hf = temp("hf", [P, 2, T], F32)
    hh = temp("hh", [P, 2, T], F16)
    hl = temp("hl", [P, 2, T], F16)
    x1 = temp("x1", [P, B, D], F32)
    x2 = temp("x2", [P, B, D], F32)
    for h in reversed(scoped):
        h.__exit__(None, None, None)
    scoped.clear()
    hn = temp("scan_hn", [P, B, D], F32)
    hnT = temp("scan_hnT", [P, C, T], F32)
    uz = temp("scan_uz", [P, T], F32)
    sg = temp("scan_sg", [ST, T], F32)
    ut = temp("scan_ut", [ST, T], F32)
    dt_ = temp("scan_dt", [ST, T], F32)
    aa = temp("scan_a", [ST, T], F32)
    bb = temp("scan_b", [ST, T], F32)
    hsn = temp("scan_h", [ST, T], F32)
    for h in reversed(scoped):
        h.__exit__(None, None, None)
    scoped.clear()
    bank = nc.alloc_psum_tensor("bank", [P, 8, 512], F32)

    def half_bank(n):
        return bank[:, n, :].bitcast(F16)

    sem = nc.alloc_semaphore
    consts = sem("consts_loaded")
    x_in = sem("x_loaded")
    kt_in = [sem("kt_loaded_0"), sem("kt_loaded_1")]
    v_in = [sem("v_loaded_0"), sem("v_loaded_1")]
    k_rep = [sem("k_stacked_0"), sem("k_stacked_1")]
    split_hi = sem("split_hi")
    split_lo = sem("split_lo")
    ones_set = sem("ones_set")
    zero_set = sem("zero_set")
    chain = sem("vector_chain")
    ln1_var = sem("ln1_var")
    roots = sem("roots")
    xn_done = sem("xn_done")
    xb_done = sem("x_plus_b_proj")
    win_done = sem("win_scaled")
    xs_step = sem("xs_step")
    m_ready = sem("max_ring_filled")
    m_taken = sem("max_ring_taken")
    mx_step = sem("max_step")
    st_done = sem("scores_ready")
    exp_done = sem("exp_done")
    add_done = sem("pair_sums_ready")
    pv_done = sem("pv_done")
    den_done = sem("den_done")
    o_ready = sem("o_ready")
    o_rd = sem("o_reciprocal")
    o_free = sem("o_taken")
    proj_done = sem("proj_done")
    x1_done = sem("x1_done")
    x1b_done = sem("x1_plus_b_out")
    ln2_var = sem("ln2_var")
    ln2_ms = sem("ln2_mean_square")
    hn_done = sem("hn_done")
    h_done = sem("h_done")
    x2p_done = sem("x2_residual")
    hnT_ready = sem("hnT_ready")
    hnT_act = sem("hnT_copied_scalar")
    hnT_dve = sem("hnT_copied_vector")
    uz_ready = sem("uz_ready")
    g_ready = sem("g_ready")
    uz_done = sem("uz_copied")
    sg_done = sem("sg_done")
    dt_ready = sem("dt_ready")
    ut_ready = sem("ut_ready")
    dt_done = sem("dt_done")
    ut_done = sem("ut_done")
    y_done = sem("y_done")
    scan_out = sem("scan_out_ready")
    x2_done = sem("x2_done")
    ln3_var = sem("ln3_var")
    h3_done = sem("h3_done")
    h3T_ready = sem("h3T_ready")
    xh_done = sem("xh_done")
    xl_done = sem("xl_done")
    gw_split = sem("router_weights_split")
    log_ready = sem("logits_ready")
    log_sub = sem("logits_minus_max")
    log_exp = sem("logits_exp")
    g20_done = sem("gates_split")
    gT_ready = sem("gates_transposed")
    gT_done = sem("gates_transposed_copied")
    gate_ready = sem("gate_spread")
    gate_act = sem("gate_copied_scalar")
    gate_dve = sem("gate_copied_vector")
    w_in = [[sem(f"w{m}_loaded_{q}") for m in range(3)] for q in range(2)]
    w_hi = sem("w_hi")
    w_lo = sem("w_lo")
    ab_ready = sem("up_ready")
    sil_done = sem("silu_done")
    mul_done = sem("mul_done")
    h_full = sem("h_full")
    h_hi = sem("h_hi")
    h_lo = sem("h_lo")
    down_done = sem("down_done")
    x3_done = sem("x3_done")
    stored = sem("stored")

    def at(i, off):
        return 2 * i + off

    def uses(i, off):
        return i + off // 2 + 1

    def run_groups(eng, body):
        body(0, 0, G)
        with eng.Fori(0, (G - 4) // 2) as i:
            body(i, 1, None)
            body(i, 2, None)
        for n in range(G - 3, G):
            body(0, n, G)

    def run_units(eng, body):
        body(0, 0, U)
        with eng.Fori(0, (U - 2) // 2) as i:
            body(i, 1, None)
            body(i, 2, None)
        body(0, U - 1, U)

    def exists(off, total, ahead):
        return total is None or off + ahead < total

    CONSTS = [(wproj[:, :, :], "wproj"), (win[:, :, :], "win"), (normw[:, :], "normw"), (bproj[:, :], "bproj"),
              (bout[:, :], "bout"), (wx[:, :], "wx"), (wout[:, :], "wout"), (cols[:, :], "cols"),
              (gwt[:, :, :], "gwt"), (gbias[:, :, :], "gbias"), (iota[:, :], "iota"), (idf[:, :], "idf"),
              (sel[:, :, :], "sel")]

    block = nc.Block()
    blk = block.__enter__()

    @blk.sync
    def _(sp):
        def load_k(i, off):
            sp.dma_start(kt[:, off % 2, :], t["keysT"][at(i, off)]).then_inc(kt_in[off % 2], 16)

        def load_v(i, off):
            sp.dma_start(v[:, off % 2, :, :], t["vals"][at(i, off)]).then_inc(v_in[off % 2], 16)

        def stack(off):
            for src, row in ((kh, 0), (kl, HD), (kh, 2 * HD)):
                for a in range(HG):
                    sp.dma_start(kstk[row:row + HD, off % 2, a, :], src[a * HD:(a + 1) * HD, off % 2, :])\
                        .then_inc(k_rep[off % 2], 16)

        load_k(0, 0)
        sp.dma_start(x[:, :, :], t["x"]).then_inc(x_in, 16)
        sp.dma_start(idh[:, :], t["idh"]).then_inc(x_in, 16)
        sp.dma_start(kstk[KS:KM, :, :, :], t["ones"]).then_inc(x_in, 16)
        load_k(0, 1)
        load_v(0, 0)
        for dst, name in CONSTS:
            sp.dma_start(dst, t[name]).then_inc(consts, 16)
        for n in range(2):
            sp.wait_ge(split_lo, n + 1)
            stack(n)
            if n == 0:
                load_k(0, 2)

        def body(i, off, total):
            if exists(off, total, 1):
                if off > 0 or total is None:
                    sp.wait_ge(pv_done, HS * at(i, off))
                load_v(i, off + 1)
            if exists(off, total, 3):
                sp.wait_ge(split_lo, at(i, off + 2))
                load_k(i, off + 3)
            if exists(off, total, 2):
                sp.wait_ge(st_done, HS * at(i, off + 1))
                sp.wait_ge(split_lo, at(i, off + 3))
                stack(off + 2)

        body(0, 0, G)
        for u in range(2):
            for m in range(3):
                sp.dma_start(wst[:, u, m, :, :], t["ffw"][u, m]).then_inc(w_in[u][m], 16)
        with sp.Fori(0, (G - 4) // 2) as i:
            body(i, 1, None)
            body(i, 2, None)
        for n in range(G - 3, G):
            body(0, n, G)

        def load_w(i, off):
            sp.wait_ge(w_lo, 3 * at(i, off - 1))
            for m in range(3):
                sp.dma_start(wst[:, off % 2, m, :, :], t["ffw"][at(i, off), m]).then_inc(w_in[off % 2][m], 16)

        with sp.Fori(0, (U - 2) // 2) as i:
            load_w(i, 2)
            load_w(i, 3)
        for b in range(B):
            sp.wait_ge(x3_done, b + 1)
            sp.dma_start(out[b], x1[:, b, :]).then_inc(stored, 16)
        sp.wait_ge(stored, 16 * B)

    NC = 16 * len(CONSTS)

    @blk.scalar
    def _(act):
        def split_keys(i, off):
            act.wait_ge(kt_in[off % 2], 16 * uses(i, off))
            act.activation(kh[:, off % 2, :], kt[:, off % 2, :], ACT.Copy).then_inc(split_hi, 1)

        def root(ready, src, count):
            act.wait_ge(ready, 1)
            act.activation(lnv[:, src + 1, :], lnv[:, src, :], ACT.Sqrt).then_inc(roots, count)

        split_keys(0, 0)
        root(ln1_var, 0, 1)
        split_keys(0, 1)

        def body(i, off, total):
            for hs in range(HS):
                act.wait_ge(st_done, HS * at(i, off) + hs + 1)
                if not (total and off == 0 and hs < 4):
                    act.wait_ge(pv_done, HS * at(i, off) + hs - 3)
                    act.wait_ge(add_done, HS * at(i, off) + hs - 3)
                act.activation(pt[:, hs % 4, :, :, :].rearrange("p j a t -> p (j a t)"),
                               bank[:, 2 * (hs % 2):2 * (hs % 2) + 2, :].rearrange("p j n -> p (j n)"),
                               ACT.Exp, scale=SC).then_inc(exp_done, 1)
                if hs == 2 and exists(off, total, 2):
                    act.wait_ge(k_rep[off % 2], 16 * 3 * HG * uses(i, off))
                    split_keys(i, off + 2)

        run_groups(act, body)

        root(ln2_var, 0, 1)
        root(ln2_ms, 3, 1)
        for b in range(0, B, 2):
            act.wait_ge(hnT_ready, b + 1)
            act.activation(hnT[:, :, b * P:(b + 1) * P], bank[:, 4 + b, :].rearrange("p (c n) -> p c n", c=C),
                           ACT.Copy).then_inc(hnT_act, 1)
        act.wait_ge(uz_ready, 1)
        act.activation(uz[:, :], bank[:, 0, :], ACT.Identity, bias=cols[:, 0:1]).then_inc(uz_done, 1)
        act.wait_ge(g_ready, 1)
        act.activation(sg[:, :], bank[0:ST, 1, :], ACT.Sigmoid, bias=cols[0:ST, 1:2]).then_inc(sg_done, 1)
        act.wait_ge(dt_ready, 1)
        act.activation(dt_[:, :], bank[0:ST, 2, :], ACT.Sigmoid, bias=cols[0:ST, 3:4]).then_inc(dt_done, 1)
        act.wait_ge(ut_ready, 1)
        act.activation(ut[:, :], bank[0:ST, 3, :], ACT.Tanh, bias=cols[0:ST, 2:3]).then_inc(ut_done, 1)
        root(ln3_var, 0, 1)

        def split_weights(i, off, m):
            act.wait_ge(w_in[off % 2][m], 16 * uses(i, off))
            act.activation(wh[:, off % 2, m, :, :].rearrange("p c n -> p (c n)"),
                           wst[:, off % 2, m, :, :].rearrange("p c n -> p (c n)"), ACT.Copy, scale=WS)\
                .then_inc(w_hi, 1)

        for b in range(B):
            act.wait_ge(h3T_ready, b + 1)
            act.activation(xh[:, :, b * P:(b + 1) * P], bank[:, b, :].rearrange("p (c n) -> p c n", c=C),
                           ACT.Copy).then_inc(xh_done, 1)
        for m in range(3):
            split_weights(0, 0, m)
        act.wait_ge(log_sub, 1)
        act.activation(lgs[:, 1, :, :], lgs[:, 0, :, :], ACT.Exp).then_inc(log_exp, 1)
        for u in range(0, U, 2):
            act.wait_ge(gate_ready, u + 1)
            act.activation(gate[:, u, :], bank[:, 4 + u % 4, :], ACT.Copy, scale=1.0 / WS).then_inc(gate_act, 1)

        def unit(i, off, total):
            for it in range(C):
                n = it if (total and off == 0) else C * at(i, off) + it
                act.wait_ge(ab_ready, n + 1)
                if not (total and off == 0 and it < 2):
                    act.wait_ge(mul_done, n - 1)
                act.activation(sil[:, it % 2, :], bank[:, 4 + 2 * (it % 2), :], ACT.Silu, scale=1.0 / WS)\
                    .then_inc(sil_done, 1)
                act.wait_ge(h_full, n + 1)
                if not (total and off == 0 and it < 2):
                    act.wait_ge(down_done, n - 1)
                act.activation(hh[:, it % 2, :], hf[:, it % 2, :], ACT.Copy).then_inc(h_hi, 1)
                if it < 3 and exists(off, total, 1):
                    if it == 0 and not (total and off == 0):
                        act.wait_ge(down_done, n)
                    split_weights(i, off + 1, it)

        run_units(act, unit)

    @blk.gpsimd
    def _(pool):
        def split_keys(i, off, q):
            if q == 0:
                pool.wait_ge(split_hi, at(i, off) + 1)
            part = slice(q * 512, (q + 1) * 512)
            low = pool.tensor_tensor(kl[:, off % 2, part], kt[:, off % 2, part], kh[:, off % 2, part], ALU.subtract)
            if q == 3:
                low.then_inc(split_lo, 1)

        pool.memset(ones[:, :], 1.0).then_inc(ones_set, 1)
        pool.memset(zero[:, :], 0.0).then_inc(zero_set, 1)
        for n in range(2):
            for q in range(4):
                split_keys(0, n, q)
        pool.wait_ge(xn_done, B)
        pool.wait_ge(consts, NC)
        for b in range(B):
            pool.tensor_tensor(x[:, b, :], x[:, b, :], bproj[:, :], ALU.add).then_inc(xb_done, 1)

        def body(i, off, total):
            for hs in range(HS):
                pool.wait_ge(exp_done, HS * at(i, off) + hs + 1)
                if not (total and off == 0 and hs < 4):
                    pool.wait_ge(den_done, HS * at(i, off) + hs - 3)
                pool.tensor_tensor(ps2[:, hs % 4, :, :], pt[:, hs % 4, 0, :, :], pt[:, hs % 4, 1, :, :], ALU.add)\
                    .then_inc(add_done, 1)
                if 3 <= hs < 7 and exists(off, total, 2):
                    split_keys(i, off + 2, hs - 3)

        run_groups(pool, body)
        for b in range(B):
            pool.wait_ge(x1_done, b + 1)
            pool.tensor_tensor(x2[:, b, :], x1[:, b, :], bout[:, :], ALU.add).then_inc(x1b_done, 1)
        for b in range(B):
            pool.wait_ge(h_done, b + 1)
            pool.wait_ge(x1b_done, b + 1)
            pool.tensor_tensor(x2[:, b, :], x2[:, b, :], xn[:, b, :], ALU.add).then_inc(x2p_done, 1)

    @blk.vector
    def _(dve):
        links = [0]

        def link(ins):
            links[0] += 1
            ins.then_inc(chain, 1)
            dve.wait_ge(chain, links[0])

        def norm_stats(src, b):
            link(dve.bn_stats(st6[:, b, :], src[:, b, :]))
            link(dve.bn_aggr(mv[:, b, :], st6[:, b, :]))

        def token_queries(i, off):
            q = xn[:, :, :].rearrange("p b (c n) -> p (b c) n", c=C)[:, at(i, off), :]\
                .rearrange("p (a d) -> p a d", a=HG)
            z = xs[:, off % 2, :, :]
            dve.tensor_copy(z[:, :, 0:HD], q).then_inc(xs_step, 1)
            dve.tensor_copy(z[:, :, HD:2 * HD], q).then_inc(xs_step, 1)
            dve.wait_ge(xs_step, 3 * at(i, off) + 1)
            dve.tensor_tensor(z[:, :, 2 * HD:KS], q, z[:, :, 0:HD], ALU.subtract).then_inc(xs_step, 1)

        def take_queries(i, off):
            dve.wait_ge(m_ready, MT * at(i, off) + 1)
            dve.tensor_copy(q1[:, :, :], half_bank(4)[0:KS, 0:512].rearrange("k (a t) -> k a t", a=HG))\
                .then_inc(m_taken, 1)

        def take_max(i, off, k):
            a, q = (k - 1) // 4, (k - 1) % 4
            dve.wait_ge(m_ready, MT * at(i, off) + k + 1)
            dve.tensor_reduce(mx[:, a, q:q + 1], bank[:, 4 + k % 2, :], AX.X, ALU.max).then_inc(m_taken, 1)

        def shift(i, off):
            dve.wait_ge(m_taken, MT * at(i, off) + MT - 1)
            dve.tensor_reduce(negm[:, :], mx[:, :, :], AX.X, ALU.max, negate=True).then_inc(mx_step, 1)
            dve.wait_ge(mx_step, 3 * at(i, off) + 1)
            z = xs[:, off % 2, :, :]
            dve.tensor_copy(z[:, :, KS:KS + 1], negm[:, :].unsqueeze(2)).then_inc(mx_step, 1)
            dve.wait_ge(mx_step, 3 * at(i, off) + 2)
            dve.tensor_tensor(z[:, :, KS + 1:KM], negm[:, :].unsqueeze(2), z[:, :, KS:KS + 1], ALU.subtract)\
                .then_inc(mx_step, 1)

        def take_shifted(i, off):
            dve.wait_ge(m_ready, MT * at(i, off) + MT)
            if not isinstance(at(i, off), int) or off >= 2:
                dve.wait_ge(st_done, HS * at(i, off - 1))
            dve.tensor_copy(q2[:, off % 2, :, :], half_bank(5)[0:KM, 0:512].rearrange("k (a t) -> k a t", a=HG))\
                .then_inc(m_taken, 1)

        def divide(i, off):
            dve.wait_ge(o_ready, at(i, off) + 1)
            if not (isinstance(at(i, off), int) and off == 0):
                dve.wait_ge(o_free, at(i, off))
            dve.reciprocal(rden[:, :], bank[:, 6 + off % 2, P:2 * P]).then_inc(o_rd, 1)
            dve.wait_ge(o_rd, at(i, off) + 1)
            dve.tensor_tensor(ao[:, at(i, off), :], bank[:, 6 + off % 2, 0:P], rden[:, :], ALU.mult)\
                .then_inc(o_free, 1)

        dve.wait_ge(x_in, 48)
        for b in range(B):
            norm_stats(x, b)
        dve.tensor_scalar(lnv[:, 0, :], mv[:, :, 1], EPS, None, ALU.add).then_inc(ln1_var, 1)
        dve.wait_ge(roots, 1)
        link(dve.reciprocal(lnv[:, 2, :], lnv[:, 1, :]))
        for b in range(B):
            dve.tensor_scalar(xn[:, b, :], x[:, b, :], mv[:, b, 0:1], lnv[:, 2, b:b + 1], ALU.subtract, ALU.mult)\
                .then_inc(xn_done, 1)
        dve.wait_ge(xn_done, B)
        token_queries(0, 0)
        token_queries(0, 1)
        take_queries(0, 0)
        for k in range(1, MT - 1):
            take_max(0, 0, k)
        shift(0, 0)
        take_shifted(0, 0)
        dve.wait_ge(consts, NC)
        for c in range(C):
            dve.tensor_scalar(win[:, c, :], win[:, c, :], normw[:, c:c + 1], None, ALU.mult).then_inc(win_done, 1)

        def body(i, off, total):
            more = exists(off, total, 1)
            if more:
                take_queries(i, off + 1)
                for k in range(1, 5):
                    take_max(i, off + 1, k)
            if not (total and off == 0):
                divide(i, off - 1)
            if more:
                for k in range(5, MT - 1):
                    take_max(i, off + 1, k)
                shift(i, off + 1)
                if exists(off, total, 2):
                    token_queries(i, off + 2)
                take_shifted(i, off + 1)

        run_groups(dve, body)
        divide(0, G - 1)

        dve.wait_ge(xb_done, B)
        for b in range(B):
            dve.wait_ge(proj_done, b + 1)
            dve.tensor_tensor(x1[:, b, :], bank[:, b, :], x[:, b, :], ALU.add).then_inc(x1_done, 1)
            dve.wait_ge(x1_done, b + 1)
            norm_stats(x1, b)
        dve.tensor_scalar(lnv[:, 0, :], mv[:, :, 1], EPS, None, ALU.add).then_inc(ln2_var, 1)
        dve.wait_ge(roots, 2)
        link(dve.reciprocal(lnv[:, 2, :], lnv[:, 1, :]))
        link(dve.tensor_tensor(lnv[:, 5, :], mv[:, :, 1], lnv[:, 2, :], ALU.mult))
        link(dve.tensor_tensor(lnv[:, 6, :], lnv[:, 5, :], lnv[:, 2, :], ALU.mult))
        dve.tensor_scalar(lnv[:, 3, :], lnv[:, 6, :], 1e-8, None, ALU.add).then_inc(ln2_ms, 1)
        dve.wait_ge(roots, 3)
        link(dve.reciprocal(lnv[:, 5, :], lnv[:, 4, :]))
        link(dve.tensor_tensor(lnv[:, 6, :], lnv[:, 5, :], lnv[:, 2, :], ALU.mult))
        for b in range(B):
            dve.tensor_scalar(hn[:, b, :], x1[:, b, :], mv[:, b, 0:1], lnv[:, 6, b:b + 1], ALU.subtract, ALU.mult)\
                .then_inc(hn_done, 1)
        for b in range(B):
            dve.tensor_scalar(xn[:, b, :], x1[:, b, :], mv[:, b, 0:1], lnv[:, 2, b:b + 1], ALU.subtract, ALU.mult)\
                .then_inc(h_done, 1)
        for b in range(1, B, 2):
            dve.wait_ge(hnT_ready, b + 1)
            dve.tensor_copy(hnT[:, :, b * P:(b + 1) * P], bank[:, 4 + b, :].rearrange("p (c n) -> p c n", c=C))\
                .then_inc(hnT_dve, 1)

        dve.wait_ge(dt_done, 1)
        link(dve.tensor_scalar(aa[:, :], dt_[:, :], -1.0, 1.0, ALU.mult, ALU.add))
        dve.wait_ge(ut_done, 1)
        link(dve.tensor_tensor(bb[:, :], dt_[:, :], ut[:, :], ALU.mult))
        for b in range(B):
            part = slice(b * P, (b + 1) * P)
            link(dve.tensor_tensor_scan(hsn[:, part], aa[:, part], bb[:, part], 0.0, ALU.mult, ALU.add))
        dve.wait_ge(sg_done, 1)
        dve.tensor_tensor(aa[:, :], hsn[:, :], sg[:, :], ALU.mult).then_inc(y_done, 1)
        for b in range(B):
            dve.wait_ge(scan_out, b + 1)
            dve.wait_ge(x2p_done, b + 1)
            dve.tensor_tensor(x2[:, b, :], bank[:, 4 + b, :], x2[:, b, :], ALU.add).then_inc(x2_done, 1)
            dve.wait_ge(x2_done, b + 1)
            norm_stats(x2, b)
        dve.tensor_scalar(lnv[:, 0, :], mv[:, :, 1], EPS, None, ALU.add).then_inc(ln3_var, 1)
        dve.wait_ge(roots, 4)
        link(dve.reciprocal(lnv[:, 2, :], lnv[:, 1, :]))
        for b in range(B):
            dve.tensor_scalar(xn[:, b, :], x2[:, b, :], mv[:, b, 0:1], lnv[:, 2, b:b + 1], ALU.subtract, ALU.mult)\
                .then_inc(h3_done, 1)

        link(dve.tensor_copy(gwh[:, :, 0:E], gwt[:, :, :]))
        dve.tensor_tensor(gwh[:, :, E:2 * E], gwt[:, :, :], gwh[:, :, 0:E], ALU.subtract).then_inc(gw_split, 1)
        for b in range(B):
            dve.wait_ge(xh_done, b + 1)
            dve.tensor_tensor(xl[:, :, b * P:(b + 1) * P], bank[:, b, :].rearrange("p (c n) -> p c n", c=C),
                              xh[:, :, b * P:(b + 1) * P], ALU.subtract).then_inc(xl_done, 1)
        dve.wait_ge(log_ready, 1)
        lg = bank[:, 4, 0:B * E].rearrange("p (b e) -> p b e", b=B)

        def over_e(col):
            return r1[:, col, :].unsqueeze(2).broadcast_to([P, B, E])

        link(dve.tensor_reduce(r1[:, 0, :], lg, AX.X, ALU.max))
        dve.tensor_tensor(lgs[:, 0, :, :], lg, over_e(0), ALU.subtract).then_inc(log_sub, 1)
        dve.wait_ge(log_exp, 1)
        link(dve.tensor_reduce(r1[:, 1, :], lgs[:, 1, :, :], AX.X, ALU.add))
        link(dve.reciprocal(r1[:, 2, :], r1[:, 1, :]))
        link(dve.tensor_tensor(lgs[:, 2, :, :], lgs[:, 1, :, :], over_e(2), ALU.mult))
        link(dve.tensor_tensor(lgs[:, 3, :, :], lgs[:, 2, :, :], gbias[:, :, :], ALU.add))
        for b in range(B):
            link(dve.max(top[:, b, :], lgs[:, 3, b, :]))
            link(dve.max_index(topi[:, b, :], top[:, b, :], lgs[:, 3, b, :]))
        link(dve.tensor_copy(topf[:, :, :], topi[:, :, :]))
        for b in range(B):
            link(dve.tensor_scalar(lgs[:, 4, b, :], iota[:, :], topf[:, b, 0:1], None, ALU.is_equal))
            link(dve.scalar_tensor_tensor(lgs[:, 5, b, :], iota[:, :], topf[:, b, 1:2], lgs[:, 4, b, :],
                                          ALU.is_equal, ALU.add))
        link(dve.tensor_tensor(lgs[:, 0, :, :], lgs[:, 5, :, :], lgs[:, 2, :, :], ALU.mult))
        link(dve.memset(g20[:, :, E:U], 1.0))
        link(dve.memset(g20[:, :, U + E:2 * U], 0.0))
        link(dve.tensor_copy(g20[:, :, 0:E], lgs[:, 0, :, :]))
        dve.tensor_tensor(g20[:, :, U:U + E], lgs[:, 0, :, :], g20[:, :, 0:E], ALU.subtract).then_inc(g20_done, 1)
        dve.wait_ge(gT_ready, 1)
        dve.tensor_copy(gT[:, :], half_bank(5)[0:2 * U, 0:T]).then_inc(gT_done, 1)
        for u in range(1, U, 2):
            dve.wait_ge(gate_ready, u + 1)
            dve.tensor_scalar(gate[:, u, :], bank[:, 4 + u % 4, :], 1.0 / WS, None, ALU.mult).then_inc(gate_dve, 1)

        def split_weights(i, off, m):
            n = m + 1 if isinstance(at(i, off), int) and off == 0 else 3 * at(i, off) + m + 1
            dve.wait_ge(w_hi, n)
            dve.scalar_tensor_tensor(wl[:, off % 2, m, :, :].rearrange("p c n -> p (c n)"),
                                     wst[:, off % 2, m, :, :].rearrange("p c n -> p (c n)"), WS,
                                     wh[:, off % 2, m, :, :].rearrange("p c n -> p (c n)"),
                                     ALU.mult, ALU.subtract).then_inc(w_lo, 1)

        for m in range(3):
            split_weights(0, 0, m)
        dve.wait_ge(gate_act, U // 2)
        dve.wait_ge(gate_dve, U // 2)

        def unit(i, off, total):
            for it in range(C):
                n = it if (total and off == 0) else C * at(i, off) + it
                dve.wait_ge(sil_done, n + 1)
                dve.tensor_tensor(hf[:, it % 2, :], bank[:, 5 + 2 * (it % 2), :], sil[:, it % 2, :], ALU.mult)\
                    .then_inc(mul_done, 1)
                dve.wait_ge(mul_done, n + 1)
                dve.tensor_tensor(hf[:, it % 2, :], hf[:, it % 2, :], gate[:, at(i, off), :], ALU.mult)\
                    .then_inc(h_full, 1)
                dve.wait_ge(h_hi, n + 1)
                if not (total and off == 0 and it < 2):
                    dve.wait_ge(down_done, n - 1)
                dve.tensor_tensor(hl[:, it % 2, :], hf[:, it % 2, :], hh[:, it % 2, :], ALU.subtract)\
                    .then_inc(h_lo, 1)
                if it < 3 and exists(off, total, 1):
                    split_weights(i, off + 1, it)

        run_units(dve, unit)
        dve.wait_ge(down_done, C * U)
        for b in range(B):
            dve.scalar_tensor_tensor(x1[:, b, :], bank[:, b, :], 1.0 / WS, x2[:, b, :], ALU.mult, ALU.add)\
                .then_inc(x3_done, 1)

    @blk.tensor
    def _(pe):
        def queries(i, off):
            pe.wait_ge(xs_step, 3 * at(i, off) + 3)
            if not (isinstance(at(i, off), int) and off == 0):
                pe.wait_ge(m_taken, MT * at(i, off) - 1)
            for a in range(HG):
                mm = pe.transpose(half_bank(4)[0:KS, a * P:(a + 1) * P], xs[:, off % 2, a, 0:KS], idh[:, :])
            mm.then_inc(m_ready, 1)

        def max_scores(i, off, k):
            a, q = (k - 1) // 4, (k - 1) % 4
            if k == 1:
                pe.wait_ge(k_rep[off % 2], 16 * 3 * HG * uses(i, off))
                pe.wait_ge(m_taken, MT * at(i, off) + 1)
            else:
                pe.wait_ge(m_taken, MT * at(i, off) + k - 1)
            pe.matmul(bank[:, 4 + k % 2, :], q1[:, a, :], kstk[0:KS, off % 2, a, q * 512:(q + 1) * 512],
                      start=True, stop=True).then_inc(m_ready, 1)

        def shifted(i, off):
            pe.wait_ge(mx_step, 3 * at(i, off) + 3)
            pe.wait_ge(m_taken, MT * at(i, off) + MT - 2)
            for a in range(HG):
                mm = pe.transpose(half_bank(5)[0:KM, a * P:(a + 1) * P], xs[:, off % 2, a, :], idh[:, :])
            mm.then_inc(m_ready, 1)

        def scores(i, off, hs):
            if hs == 0:
                pe.wait_ge(m_taken, MT * at(i, off) + MT)
            if not (isinstance(at(i, off), int) and off == 0 and hs < 2):
                pe.wait_ge(exp_done, HS * at(i, off) + hs - 1)
            for j in range(2):
                for a in range(HG):
                    tile = 2 * hs + j
                    mm = pe.matmul(bank[:, 2 * (hs % 2) + j, a * P:(a + 1) * P],
                                   kstk[:, off % 2, a, tile * P:(tile + 1) * P], q2[:, off % 2, a, :],
                                   start=True, stop=True)
            mm.then_inc(st_done, 1)

        def values(i, off, hs):
            pe.wait_ge(exp_done, HS * at(i, off) + hs + 1)
            if hs == 0:
                pe.wait_ge(v_in[off % 2], 16 * uses(i, off))
                if not (isinstance(at(i, off), int) and off < 2):
                    pe.wait_ge(o_free, at(i, off - 1))
            for j in range(2):
                for a in range(HG):
                    tile = 2 * hs + j
                    mm = pe.matmul(bank[a * HD:(a + 1) * HD, 6 + off % 2, 0:P], v[:, off % 2, tile, a * HD:(a + 1) * HD],
                                   pt[:, hs % 4, j, a, :], start=(tile == 0), stop=(tile == J - 1),
                                   skip_group_check=True)
            mm.then_inc(pv_done, 1)

        def denominators(i, off, hs):
            pe.wait_ge(add_done, HS * at(i, off) + hs + 1)
            for a in range(HG):
                mm = pe.matmul(bank[a * HD:(a + 1) * HD, 6 + off % 2, P:2 * P], ones[:, :], ps2[:, hs % 4, a, :],
                               start=False, stop=(hs == HS - 1), skip_group_check=True)
            mm.then_inc(den_done, 1)
            if hs == HS - 1:
                pe.wait_ge(den_done, HS * at(i, off) + HS)
                pe.nop().then_inc(o_ready, 1)

        pe.wait_ge(ones_set, 1)
        pe.wait_ge(x_in, 48)
        queries(0, 0)
        for k in range(1, MT - 1):
            max_scores(0, 0, k)
        shifted(0, 0)
        scores(0, 0, 0)

        SPREAD = {1: range(1, 4), 2: range(4, 7), 3: range(7, 10), 4: range(10, 13), 5: range(13, 17)}

        def body(i, off, total):
            more = exists(off, total, 1)
            for hs in range(HS):
                if hs + 1 < HS:
                    scores(i, off, hs + 1)
                elif more:
                    scores(i, off + 1, 0)
                if more:
                    if hs == 0:
                        queries(i, off + 1)
                    for k in SPREAD.get(hs, ()):
                        max_scores(i, off + 1, k)
                values(i, off, hs)
                if hs > 0:
                    denominators(i, off, hs - 1)
                elif not (total and off == 0):
                    denominators(i, off - 1, HS - 1)
                if hs == 6 and more:
                    shifted(i, off + 1)

        run_groups(pe, body)
        denominators(0, G - 1, HS - 1)

        pe.wait_ge(consts, NC)
        pe.wait_ge(o_free, G)
        for b in range(B):
            for c in range(C):
                mm = pe.matmul(bank[:, b, :], ao[:, C * b + c, :], wproj[:, c, :], start=(c == 0), stop=(c == C - 1))
            mm.then_inc(proj_done, 1)

        for b in range(B):
            pe.wait_ge(hn_done, b + 1)
            for c in range(C):
                mm = pe.transpose(bank[:, 4 + b, c * P:(c + 1) * P], hn[:, b, c * P:(c + 1) * P], idf[:, :])
            mm.then_inc(hnT_ready, 1)
        pe.wait_ge(hnT_act, B // 2)
        pe.wait_ge(hnT_dve, B // 2)
        pe.wait_ge(win_done, C)
        pe.wait_ge(x1_done, B)
        for c in range(C):
            mm = pe.matmul(bank[:, 0, :], win[:, c, 0:2 * ST], hnT[:, c, :], start=(c == 0), stop=(c == C - 1))
        mm.then_inc(uz_ready, 1)
        for c in range(C):
            mm = pe.matmul(bank[0:ST, 1, :], win[:, c, 2 * ST:3 * ST], hnT[:, c, :], start=(c == 0), stop=(c == C - 1))
        mm.then_inc(g_ready, 1)
        pe.wait_ge(uz_done, 1)
        pe.matmul(bank[0:ST, 2, :], wx[ST:2 * ST, :], uz[ST:2 * ST, :], start=True, stop=True).then_inc(dt_ready, 1)
        pe.matmul(bank[0:ST, 3, :], wx[0:ST, :], uz[0:ST, :], start=True, stop=True).then_inc(ut_ready, 1)
        pe.wait_ge(y_done, 1)
        for b in range(B):
            pe.matmul(bank[:, 4 + b, :], aa[:, b * P:(b + 1) * P], wout[:, :], start=True, stop=True)\
                .then_inc(scan_out, 1)

        for b in range(B):
            pe.wait_ge(h3_done, b + 1)
            for c in range(C):
                mm = pe.transpose(bank[:, b, c * P:(c + 1) * P], xn[:, b, c * P:(c + 1) * P], idf[:, :])
            mm.then_inc(h3T_ready, 1)
        pe.wait_ge(gw_split, 1)
        for b in range(B):
            part = slice(b * P, (b + 1) * P)
            pe.wait_ge(xl_done, b + 1)
            for c in range(C):
                pe.matmul(bank[:, 4, b * E:(b + 1) * E], xh[:, c, part], gwh[:, c, 0:E], start=(c == 0), stop=False)
                pe.matmul(bank[:, 4, b * E:(b + 1) * E], xh[:, c, part], gwh[:, c, E:2 * E], start=False, stop=False)
                mm = pe.matmul(bank[:, 4, b * E:(b + 1) * E], xl[:, c, part], gwh[:, c, 0:E], start=False,
                               stop=(c == C - 1))
        mm.then_inc(log_ready, 1)
        pe.wait_ge(zero_set, 1)
        for b in range(B):
            pe.matmul(bank[:, b, :], zero[:, 0:P], zero[:, :], start=True, stop=False, skip_group_check=True)
        pe.wait_ge(g20_done, 1)
        for b in range(B):
            mm = pe.transpose(half_bank(5)[0:2 * U, b * P:(b + 1) * P], g20[:, b, :], idh[:, :])
        mm.then_inc(gT_ready, 1)
        pe.wait_ge(gT_done, 1)
        for u in range(U):
            if u >= 4:
                pe.wait_ge((gate_act, gate_dve)[u % 2], (u - 4) // 2 + 1)
            pe.matmul(bank[:, 4 + u % 4, :], sel[:, u, :], gT[:, :], start=True, stop=True).then_inc(gate_ready, 1)
        pe.wait_ge(gate_act, U // 2)
        pe.wait_ge(gate_dve, U // 2)

        def up(i, off, it, n):
            part = slice(it * P, (it + 1) * P)
            q = off % 2
            for m in range(2):
                for c in range(C):
                    o = bank[:, 4 + 2 * (it % 2) + m, :]
                    pe.matmul(o, wh[:, q, m, c, part], xh[:, c, :], start=(c == 0), stop=False)
                    pe.matmul(o, wh[:, q, m, c, part], xl[:, c, :], start=False, stop=False)
                    mm = pe.matmul(o, wl[:, q, m, c, part], xh[:, c, :], start=False, stop=(c == C - 1))
            mm.then_inc(ab_ready, 1)

        def down(q, it, n):
            pe.wait_ge(h_hi, n)
            pe.wait_ge(h_lo, n)
            for b in range(B):
                part = slice(b * P, (b + 1) * P)
                pe.matmul(bank[:, b, :], hh[:, it % 2, part], wh[:, q, 2, it, :], start=False, stop=False,
                          skip_group_check=True)
                pe.matmul(bank[:, b, :], hh[:, it % 2, part], wl[:, q, 2, it, :], start=False, stop=False,
                          skip_group_check=True)
                mm = pe.matmul(bank[:, b, :], hl[:, it % 2, part], wh[:, q, 2, it, :], start=False, stop=False,
                               skip_group_check=True)
            mm.then_inc(down_done, 1)

        def unit(i, off, total):
            first = total and off == 0
            for it in range(C):
                n = it if first else C * at(i, off) + it
                if it == 0:
                    pe.wait_ge(w_hi, 3 * at(i, off) + 2)
                    pe.wait_ge(w_lo, 3 * at(i, off) + 2)
                if not (first and it < 2):
                    pe.wait_ge(mul_done, n - 1)
                up(i, off, it, n)
                if it == 0:
                    if not first:
                        down((off - 1) % 2, C - 1, n)
                else:
                    if it == 1:
                        pe.wait_ge(w_hi, 3 * at(i, off) + 3)
                        pe.wait_ge(w_lo, 3 * at(i, off) + 3)
                    down(off % 2, it - 1, n)

        run_units(pe, unit)
        down((U - 1) % 2, C - 1, C * U)

    block.__exit__(None, None, None)


def kernel(**inputs):
    import concourse.bacc as bacc
    from concourse.bass_utils import run_bass_kernel_spmd

    a = {k.replace("L0_", ""): np.asarray(v) for k, v in inputs.items()}
    ctx = a["ctx_1024"]
    def rows(w):
        w = w.reshape(*w.shape[:-2], w.shape[-2] // P, P, w.shape[-1])
        return np.moveaxis(w, -2, -3)

    def spread(row):
        return np.broadcast_to(row, (P, *row.shape))

    w1 = np.concatenate([a["ffn_w1"], a["ffn_sw1"].reshape(2, D, D)])
    w3 = np.concatenate([a["ffn_w3"], a["ffn_sw3"].reshape(2, D, D)])
    w2 = np.concatenate([a["ffn_w2"], a["ffn_sw2"].reshape(D, 2, D).transpose(1, 0, 2)])
    ffw = np.stack([rows(w.transpose(0, 2, 1)) for w in (w1, w3, w2)], axis=1)
    cols = np.zeros((P, 4), np.float32)
    cols[:, 0] = a["attn_b_in"][:P]
    cols[:ST, 1] = a["attn_b_in"][P:]
    cols[:ST, 2] = a["attn_b_x"]
    cols[:ST, 3] = a["attn_b_dt"]
    pick = np.concatenate([np.eye(U), np.eye(U)]).astype(np.float16)
    arrays = {
        "x": a["x"].transpose(1, 0, 2),
        "keysT": ctx.transpose(0, 2, 1).reshape(G, P, S),
        "vals": ctx.reshape(B, J, P, C, P).transpose(0, 3, 2, 1, 4).reshape(G, P, J, P),
        "ffw": ffw,
        "wproj": rows(a["xattn_w_proj"].T),
        "win": rows(a["attn_W_in"]),
        "normw": a["attn_norm_w"].reshape(C, P).T,
        "bproj": spread(a["xattn_b_proj"]),
        "bout": spread(a["attn_b_out"]),
        "wx": np.concatenate([a["attn_W_x"], a["attn_W_dt"]]),
        "wout": a["attn_W_out"],
        "cols": cols,
        "gwt": rows(a["ffn_gate_w"].T),
        "gbias": spread(np.broadcast_to(a["ffn_gate_bias"], (B, E))),
        "iota": spread(np.arange(E, dtype=np.float32)),
        "idf": np.eye(P, dtype=np.float32),
        "idh": np.eye(P, dtype=np.float16),
        "ones": np.ones((KM - KS, 2, HG, S), np.float16),
        "sel": np.broadcast_to(pick[:, :, None], (2 * U, U, P)),
    }
    nc = bacc.Bacc("TRN2", target_bir_lowering=False, num_devices=1)
    feed, aps = {}, {}
    for name, arr in arrays.items():
        arr = np.ascontiguousarray(arr)
        feed[f"in_{name}"] = arr
        aps[name] = nc.dram_tensor(f"in_{name}", arr.shape, mybir.dt.from_np(arr.dtype), kind="ExternalInput").ap()
    out = nc.dram_tensor("out_0", (B, P, D), F32, kind="ExternalOutput").ap()
    build_program(nc, aps, out)
    r = run_bass_kernel_spmd(nc, [feed], core_ids=[0])
    return r.results[0]["out_0"]
```

```python
import concourse.bass as bass
from concourse import mybir
import numpy as np

F32 = mybir.dt.float32
F16 = mybir.dt.float16
U32 = mybir.dt.uint32
ALU = mybir.AluOpType
ACT = mybir.ActivationFunctionType
AX = mybir.AxisListType

P = 128
B = 4
D = 512
C = D // P
S = 2048
J = S // P
HD = 32
HG = P // HD
G = B * C
T = B * P
ST = 64
E = 8
U = E + 2
HS = J // 2
MT = 2 + HG * HG
KS = 3 * HD
KM = KS + 2
SC = float(HD) ** -0.5
EPS = 1e-5
WS = 16.0


def build_program(nc, t, out):
    sb = nc.alloc_sbuf_tensor
    scoped = []

    def temp(name, shape, dt):
        h = nc.sbuf_tensor(name, shape, dt)
        scoped.append(h)
        return h.__enter__()

    x = sb("x_tok", [P, B, D], F32)
    xn = sb("xn", [P, B, D], F32)
    ao = sb("ao", [P, G, P], F32)
    wproj = sb("wproj", [P, C, D], F32)
    win = sb("win", [P, C, 3 * ST], F32)
    normw = sb("normw", [P, C], F32)
    bproj = sb("bproj", [P, D], F32)
    bout = sb("bout", [P, D], F32)
    wx = sb("wx", [P, ST], F32)
    wout = sb("wout", [ST, D], F32)
    cols = sb("cols", [P, 4], F32)
    gwt = sb("gwt", [P, C, E], F32)
    gbias = sb("gbias", [P, B, E], F32)
    iota = sb("iota", [P, E], F32)
    idf = sb("idf", [P, P], F32)
    idh = sb("idh", [P, P], F16)
    sel = sb("sel", [2 * U, U, P], F16)
    wst = sb("wst", [P, 2, 3, C, D], F32)
    zero = sb("zero", [P, 512], F16)
    mv = sb("mv", [P, B, 2], F32)
    st6 = sb("st6", [P, B, 6], F32)
    lnv = sb("lnv", [P, 8, B], F32)

    gwh = sb("gwh", [P, C, 2 * E], F16)
    lgs = sb("lgs", [P, 6, B, E], F32)
    top = sb("top", [P, B, 8], F32)
    topi = sb("topi", [P, B, 8], U32)
    topf = sb("topf", [P, B, 8], F32)
    r1 = sb("r1", [P, 3, B], F32)
    g20 = sb("g20", [P, B, 2 * U], F16)
    gT = sb("gT", [2 * U, T], F16)

    kt = temp("kt", [P, 2, HG, S // 4], F32)
    kh = temp("kh", [P, 2, HG, S // 4], F16)
    kl = temp("kl", [P, 2, HG, S // 4], F16)
    kstk = temp("kstk", [KM, 2, HG, S], F16)
    v = temp("v", [P, 2, J, P], F32)
    pt = temp("pt", [P, 4, 2, HG, P], F32)
    ps2 = temp("ps2", [P, 4, HG, P], F32)
    xs = temp("xs", [P, 2, HG, KM], F16)
    q1 = temp("q1", [KS, HG, P], F16)
    q2 = temp("q2", [KM, 2, HG, P], F16)
    mx = temp("mx", [P, HG, HG], F32)
    negm = temp("negm", [P, HG], F32)
    rden = temp("rden", [P, P], F32)
    ones = temp("ones", [P, HD], F32)
    for h in reversed(scoped):
        h.__exit__(None, None, None)
    scoped.clear()

    wh = temp("wh", [P, 2, 3, C, D], F16)
    wl = temp("wl", [P, 2, 3, C, D], F16)
    gate = temp("gate", [P, U, T], F32)
    xh = temp("xh", [P, C, T], F16)
    xl = temp("xl", [P, C, T], F16)
    sil = temp("sil", [P, 2, T], F32)
    hf = temp("hf", [P, 2, T], F32)
    hh = temp("hh", [P, 2, T], F16)
    hl = temp("hl", [P, 2, T], F16)
    x1 = temp("x1", [P, B, D], F32)
    x2 = temp("x2", [P, B, D], F32)
    for h in reversed(scoped):
        h.__exit__(None, None, None)
    scoped.clear()
    hn = temp("scan_hn", [P, B, D], F32)
    hnT = temp("scan_hnT", [P, C, T], F32)
    uz = temp("scan_uz", [P, T], F32)
    sg = temp("scan_sg", [ST, T], F32)
    ut = temp("scan_ut", [ST, T], F32)
    dt_ = temp("scan_dt", [ST, T], F32)
    aa = temp("scan_a", [ST, T], F32)
    bb = temp("scan_b", [ST, T], F32)
    hsn = temp("scan_h", [ST, T], F32)
    for h in reversed(scoped):
        h.__exit__(None, None, None)
    scoped.clear()
    bank = nc.alloc_psum_tensor("bank", [P, 8, 512], F32)

    def half_bank(n):
        return bank[:, n, :].bitcast(F16)

    sem = nc.alloc_semaphore
    consts = sem("consts_loaded")
    x_in = sem("x_loaded")
    x0_in = sem("x_first_batch_loaded")
    id_in = sem("identity_and_ones_loaded")
    kt_in = [sem("kt_loaded_0"), sem("kt_loaded_1")]
    v_in = [sem("v_loaded_0"), sem("v_loaded_1")]
    k_rep = [[sem(f"k_stacked_{q}_{h}") for h in range(2)] for q in range(2)]
    split_hi = sem("split_hi")
    split_lo = sem("split_lo")
    lo_dve = sem("split_lo_by_vector")
    ones_set = sem("ones_set")
    zero_set = sem("zero_set")
    chain = sem("vector_chain")
    ln1_var = sem("ln1_var")
    roots = sem("roots")
    xn_done = sem("xn_done")
    xb_done = sem("x_plus_b_proj")
    win_done = sem("win_scaled")
    xs_step = sem("xs_step")
    m_ready = sem("max_ring_filled")
    m_taken = sem("max_ring_taken")
    mx_step = sem("max_step")
    st_done = sem("scores_ready")
    exp_done = sem("exp_done")
    add_done = sem("pair_sums_ready")
    pv_done = sem("pv_done")
    den_done = sem("den_done")
    o_ready = sem("o_ready")
    o_rd = sem("o_reciprocal")
    o_free = sem("o_taken")
    proj_done = sem("proj_done")
    x1_done = sem("x1_done")
    x1b_done = sem("x1_plus_b_out")
    ln2_var = sem("ln2_var")
    ln2_ms = sem("ln2_mean_square")
    hn_done = sem("hn_done")
    h_done = sem("h_done")
    x2p_done = sem("x2_residual")
    hnT_ready = sem("hnT_ready")
    hnT_act = sem("hnT_copied_scalar")
    hnT_dve = sem("hnT_copied_vector")
    uz_ready = sem("uz_ready")
    g_ready = sem("g_ready")
    uz_done = sem("uz_copied")
    sg_done = sem("sg_done")
    dt_ready = sem("dt_ready")
    ut_ready = sem("ut_ready")
    dt_done = sem("dt_done")
    ut_done = sem("ut_done")
    y_done = sem("y_done")
    scan_out = sem("scan_out_ready")
    x2_done = sem("x2_done")
    ln3_var = sem("ln3_var")
    h3_done = sem("h3_done")
    h3T_ready = sem("h3T_ready")
    xh_done = sem("xh_done")
    xl_done = sem("xl_done")
    gw_split = sem("router_weights_split")
    log_ready = sem("logits_ready")
    log_sub = sem("logits_minus_max")
    log_exp = sem("logits_exp")
    g20_done = sem("gates_split")
    gT_ready = sem("gates_transposed")
    gT_done = sem("gates_transposed_copied")
    gate_ready = sem("gate_spread")
    gate_act = sem("gate_copied_scalar")
    gate_dve = sem("gate_copied_vector")
    w_in = [[sem(f"w{m}_loaded_{q}") for m in range(3)] for q in range(2)]
    w_hi = sem("w_hi")
    w_lo = sem("w_lo")
    ab_ready = sem("up_ready")
    sil_done = sem("silu_done")
    mul_done = sem("mul_done")
    h_full = sem("h_full")
    h_hi = sem("h_hi")
    h_lo = sem("h_lo")
    down_done = sem("down_done")
    x3_done = sem("x3_done")
    stored = sem("stored")

    def at(i, off):
        return 2 * i + off

    def uses(i, off):
        return i + off // 2 + 1

    def run_groups(eng, body, before_last=None):
        body(0, 0, G)
        with eng.Fori(0, (G - 4) // 2) as i:
            body(i, 1, None)
            body(i, 2, None)
        body(0, G - 3, G)
        body(0, G - 2, G)
        if before_last:
            before_last()
        body(0, G - 1, G)

    def run_units(eng, body):
        body(0, 0, U)
        with eng.Fori(0, (U - 2) // 2) as i:
            body(i, 1, None)
            body(i, 2, None)
        body(0, U - 1, U)

    def exists(off, total, ahead):
        return total is None or off + ahead < total

    def block_of(k):
        h, k = divmod(k - 1, 2 * HG)
        return k // 2, 2 * h + k % 2

    CONSTS = [(wproj[:, :, :], "wproj"), (win[:, :, :], "win"), (normw[:, :], "normw"), (bproj[:, :], "bproj"),
              (bout[:, :], "bout"), (wx[:, :], "wx"), (wout[:, :], "wout"), (cols[:, :], "cols"),
              (gwt[:, :, :], "gwt"), (gbias[:, :, :], "gbias"), (iota[:, :], "iota"), (idf[:, :], "idf"),
              (sel[:, :, :], "sel")]

    block = nc.Block()
    blk = block.__enter__()

    @blk.sync
    def _(sp):
        def load_k(i, off):
            sp.dma_start(kt[:, off % 2, :, :], t["keysT"][at(i, off)]).then_inc(kt_in[off % 2], 16)

        def load_v(i, off):
            sp.dma_start(v[:, off % 2, :, :], t["vals"][at(i, off)]).then_inc(v_in[off % 2], 16)

        def copies(off, h, src, rows):
            for row in rows:
                for q in (2 * h, 2 * h + 1):
                    sp.dma_start(kstk[row:row + HD, off % 2, :, q * S // 4:(q + 1) * S // 4],
                                 src[q * HD:(q + 1) * HD, off % 2, :, :]).then_inc(k_rep[off % 2][h], 16)

        def stack(off, h):
            copies(off, h, kh, (0, 2 * HD))
            copies(off, h, kl, (HD,))

        sp.dma_start(x[:, 0, :], t["x"][:, 0, :]).then_inc(x0_in, 16)
        load_k(0, 0)
        sp.dma_start(idh[:, :], t["idh"]).then_inc(id_in, 16)
        sp.dma_start(kstk[KS:KM, :, :, :], t["ones"]).then_inc(id_in, 16)
        sp.dma_start(x[:, 1:B, :], t["x"][:, 1:B, :]).then_inc(x_in, 16)
        load_k(0, 1)
        sp.wait_ge(split_hi, 1)
        for h in range(2):
            copies(0, h, kh, (0, 2 * HD))
        sp.wait_ge(lo_dve, 1)
        sp.wait_ge(split_lo, 1)
        for h in range(2):
            copies(0, h, kl, (HD,))
        load_v(0, 0)
        load_k(0, 2)
        sp.wait_ge(split_lo, 2)
        stack(1, 0)
        stack(1, 1)

        def body(i, off, total):
            if exists(off, total, 3):
                sp.wait_ge(split_lo, at(i, off + 2))
                load_k(i, off + 3)
            if exists(off, total, 1):
                if off > 0 or total is None:
                    sp.wait_ge(pv_done, HS * at(i, off))
                load_v(i, off + 1)
            if exists(off, total, 2):
                sp.wait_ge(st_done, HS * at(i, off) + HS // 2)
                sp.wait_ge(split_lo, at(i, off + 3))
                stack(off + 2, 0)
                sp.wait_ge(st_done, HS * at(i, off + 1))
                stack(off + 2, 1)

        body(0, 0, G)
        with sp.Fori(0, (G - 4) // 2) as i:
            body(i, 1, None)
            body(i, 2, None)
        body(0, G - 3, G)
        for dst, name in CONSTS:
            sp.dma_start(dst, t[name]).then_inc(consts, 16)
        body(0, G - 2, G)
        for u in range(2):
            for m in range(3):
                sp.dma_start(wst[:, u, m, :, :], t["ffw"][u, m]).then_inc(w_in[u][m], 16)
        body(0, G - 1, G)

        def load_w(i, off):
            sp.wait_ge(w_lo, 3 * at(i, off - 1))
            for m in range(3):
                sp.dma_start(wst[:, off % 2, m, :, :], t["ffw"][at(i, off), m]).then_inc(w_in[off % 2][m], 16)

        with sp.Fori(0, (U - 2) // 2) as i:
            load_w(i, 2)
            load_w(i, 3)
        for b in range(B):
            sp.wait_ge(x3_done, b + 1)
            sp.dma_start(out[b], x1[:, b, :]).then_inc(stored, 16)
        sp.wait_ge(stored, 16 * B)

    NC = 16 * len(CONSTS)

    @blk.scalar
    def _(act):
        def split_keys(i, off):
            act.wait_ge(kt_in[off % 2], 16 * uses(i, off))
            act.activation(kh[:, off % 2, :, :].rearrange("p a s -> p (a s)"),
                           kt[:, off % 2, :, :].rearrange("p a s -> p (a s)"), ACT.Copy).then_inc(split_hi, 1)

        def root(ready, count, src, b0=0):
            act.wait_ge(ready, count)
            act.activation(lnv[:, src + 1, b0:], lnv[:, src, b0:], ACT.Sqrt).then_inc(roots, 1)

        split_keys(0, 0)
        act.wait_ge(ln1_var, 1)
        act.activation(lnv[:, 1, 0:1], lnv[:, 0, 0:1], ACT.Sqrt).then_inc(roots, 1)
        root(ln1_var, 2, 0, 1)
        split_keys(0, 1)
        for h in range(2):
            act.wait_ge(k_rep[0][h], 16 * 6)
        split_keys(0, 2)

        def body(i, off, total):
            for hs in range(HS):
                act.wait_ge(st_done, HS * at(i, off) + hs + 1)
                if not (total and off == 0 and hs < 4):
                    act.wait_ge(pv_done, HS * at(i, off) + hs - 3)
                    act.wait_ge(add_done, HS * at(i, off) + hs - 3)
                act.activation(pt[:, hs % 4, :, :, :].rearrange("p j a t -> p (j a t)"),
                               bank[:, 2 * (hs % 2):2 * (hs % 2) + 2, :].rearrange("p j n -> p (j n)"),
                               ACT.Exp, scale=SC).then_inc(exp_done, 1)
                if hs == HS // 2 - 1 and exists(off, total, 3):
                    for h in range(2):
                        act.wait_ge(k_rep[(off + 1) % 2][h], 16 * 6 * uses(i, off + 1))
                    split_keys(i, off + 3)

        run_groups(act, body)

        root(ln2_var, 1, 0)
        root(ln2_ms, 1, 3)
        for b in range(0, B, 2):
            act.wait_ge(hnT_ready, b + 1)
            act.activation(hnT[:, :, b * P:(b + 1) * P], bank[:, 4 + b, :].rearrange("p (c n) -> p c n", c=C),
                           ACT.Copy).then_inc(hnT_act, 1)
        act.wait_ge(uz_ready, 1)
        act.activation(uz[:, :], bank[:, 0, :], ACT.Identity, bias=cols[:, 0:1]).then_inc(uz_done, 1)
        act.wait_ge(g_ready, 1)
        act.activation(sg[:, :], bank[0:ST, 1, :], ACT.Sigmoid, bias=cols[0:ST, 1:2]).then_inc(sg_done, 1)
        act.wait_ge(dt_ready, 1)
        act.activation(dt_[:, :], bank[0:ST, 2, :], ACT.Sigmoid, bias=cols[0:ST, 3:4]).then_inc(dt_done, 1)
        act.wait_ge(ut_ready, 1)
        act.activation(ut[:, :], bank[0:ST, 3, :], ACT.Tanh, bias=cols[0:ST, 2:3]).then_inc(ut_done, 1)
        root(ln3_var, 1, 0)

        def split_weights(i, off, m):
            act.wait_ge(w_in[off % 2][m], 16 * uses(i, off))
            act.activation(wh[:, off % 2, m, :, :].rearrange("p c n -> p (c n)"),
                           wst[:, off % 2, m, :, :].rearrange("p c n -> p (c n)"), ACT.Copy, scale=WS)\
                .then_inc(w_hi, 1)

        for b in range(B):
            act.wait_ge(h3T_ready, b + 1)
            act.activation(xh[:, :, b * P:(b + 1) * P], bank[:, b, :].rearrange("p (c n) -> p c n", c=C),
                           ACT.Copy).then_inc(xh_done, 1)
        for m in range(3):
            split_weights(0, 0, m)
        act.wait_ge(log_sub, 1)
        act.activation(lgs[:, 1, :, :], lgs[:, 0, :, :], ACT.Exp).then_inc(log_exp, 1)
        for u in range(0, U, 2):
            act.wait_ge(gate_ready, u + 1)
            act.activation(gate[:, u, :], bank[:, 4 + u % 4, :], ACT.Copy, scale=1.0 / WS).then_inc(gate_act, 1)

        def unit(i, off, total):
            for it in range(C):
                n = it if (total and off == 0) else C * at(i, off) + it
                act.wait_ge(ab_ready, n + 1)
                if not (total and off == 0 and it < 2):
                    act.wait_ge(mul_done, n - 1)
                act.activation(sil[:, it % 2, :], bank[:, 4 + 2 * (it % 2), :], ACT.Silu, scale=1.0 / WS)\
                    .then_inc(sil_done, 1)
                act.wait_ge(h_full, n + 1)
                if not (total and off == 0 and it < 2):
                    act.wait_ge(down_done, n - 1)
                act.activation(hh[:, it % 2, :], hf[:, it % 2, :], ACT.Copy).then_inc(h_hi, 1)
                if it < 3 and exists(off, total, 1):
                    if it == 0 and not (total and off == 0):
                        act.wait_ge(down_done, n)
                    split_weights(i, off + 1, it)

        run_units(act, unit)

    @blk.gpsimd
    def _(pool):
        def split_keys(i, off, a):
            if a == 0:
                pool.wait_ge(split_hi, at(i, off) + 1)
            low = pool.tensor_tensor(kl[:, off % 2, a, :], kt[:, off % 2, a, :], kh[:, off % 2, a, :], ALU.subtract)
            if a == HG - 1:
                low.then_inc(split_lo, 1)

        pool.memset(ones[:, :], 1.0).then_inc(ones_set, 1)
        pool.memset(zero[:, :], 0.0).then_inc(zero_set, 1)
        pool.wait_ge(split_hi, 1)
        for a in range(2, HG):
            split_keys(0, 0, a)
        for n in range(1, 3):
            for a in range(HG):
                split_keys(0, n, a)

        def body(i, off, total):
            for hs in range(HS):
                pool.wait_ge(exp_done, HS * at(i, off) + hs + 1)
                if not (total and off == 0 and hs < 4):
                    pool.wait_ge(den_done, HS * at(i, off) + hs - 3)
                pool.tensor_tensor(ps2[:, hs % 4, :, :], pt[:, hs % 4, 0, :, :], pt[:, hs % 4, 1, :, :], ALU.add)\
                    .then_inc(add_done, 1)
                if hs >= HS - HG and exists(off, total, 3):
                    split_keys(i, off + 3, hs - (HS - HG))

        def add_bias():
            pool.wait_ge(xn_done, B)
            pool.wait_ge(consts, NC)
            for b in range(B):
                pool.tensor_tensor(x[:, b, :], x[:, b, :], bproj[:, :], ALU.add).then_inc(xb_done, 1)

        run_groups(pool, body)
        add_bias()
        for b in range(B):
            pool.wait_ge(x1_done, b + 1)
            pool.tensor_tensor(x2[:, b, :], x1[:, b, :], bout[:, :], ALU.add).then_inc(x1b_done, 1)
        for b in range(B):
            pool.wait_ge(h_done, b + 1)
            pool.wait_ge(x1b_done, b + 1)
            pool.tensor_tensor(x2[:, b, :], x2[:, b, :], xn[:, b, :], ALU.add).then_inc(x2p_done, 1)

    @blk.vector
    def _(dve):
        links = [0]

        def link(ins):
            links[0] += 1
            ins.then_inc(chain, 1)
            dve.wait_ge(chain, links[0])

        def norm_stats(src, b):
            link(dve.bn_stats(st6[:, b, :], src[:, b, :]))
            link(dve.bn_aggr(mv[:, b, :], st6[:, b, :]))

        def token_queries(i, off):
            q = xn[:, :, :].rearrange("p b (c n) -> p (b c) n", c=C)[:, at(i, off), :]\
                .rearrange("p (a d) -> p a d", a=HG)
            z = xs[:, off % 2, :, :]
            dve.tensor_copy(z[:, :, 0:HD], q).then_inc(xs_step, 1)
            dve.tensor_copy(z[:, :, HD:2 * HD], q).then_inc(xs_step, 1)
            dve.wait_ge(xs_step, 3 * at(i, off) + 1)
            dve.tensor_tensor(z[:, :, 2 * HD:KS], q, z[:, :, 0:HD], ALU.subtract).then_inc(xs_step, 1)

        def take_queries(i, off):
            dve.wait_ge(m_ready, MT * at(i, off) + 1)
            dve.tensor_copy(q1[:, :, :], half_bank(4)[0:KS, 0:512].rearrange("k (a t) -> k a t", a=HG))\
                .then_inc(m_taken, 1)

        def take_max(i, off, k):
            a, q = block_of(k)
            dve.wait_ge(m_ready, MT * at(i, off) + k + 1)
            dve.tensor_reduce(mx[:, a, q:q + 1], bank[:, 4 + k % 2, :], AX.X, ALU.max).then_inc(m_taken, 1)

        def shift(i, off):
            dve.wait_ge(m_taken, MT * at(i, off) + MT - 1)
            dve.tensor_reduce(negm[:, :], mx[:, :, :], AX.X, ALU.max, negate=True).then_inc(mx_step, 1)
            dve.wait_ge(mx_step, 3 * at(i, off) + 1)
            z = xs[:, off % 2, :, :]
            dve.tensor_copy(z[:, :, KS:KS + 1], negm[:, :].unsqueeze(2)).then_inc(mx_step, 1)
            dve.wait_ge(mx_step, 3 * at(i, off) + 2)
            dve.tensor_tensor(z[:, :, KS + 1:KM], negm[:, :].unsqueeze(2), z[:, :, KS:KS + 1], ALU.subtract)\
                .then_inc(mx_step, 1)

        def take_shifted(i, off):
            dve.wait_ge(m_ready, MT * at(i, off) + MT)
            if not isinstance(at(i, off), int) or off >= 2:
                dve.wait_ge(st_done, HS * at(i, off - 1))
            dve.tensor_copy(q2[:, off % 2, :, :], half_bank(5)[0:KM, 0:512].rearrange("k (a t) -> k a t", a=HG))\
                .then_inc(m_taken, 1)

        def invert(i, off):
            dve.wait_ge(o_ready, at(i, off) + 1)
            if not (isinstance(at(i, off), int) and off == 0):
                dve.wait_ge(o_free, at(i, off))
            dve.reciprocal(rden[:, :], bank[:, 6 + off % 2, P:2 * P]).then_inc(o_rd, 1)

        def divide(i, off):
            dve.wait_ge(o_rd, at(i, off) + 1)
            dve.tensor_tensor(ao[:, at(i, off), :], bank[:, 6 + off % 2, 0:P], rden[:, :], ALU.mult)\
                .then_inc(o_free, 1)

        def first_norm(b0, b1):
            for b in range(b0, b1):
                norm_stats(x, b)
            dve.tensor_scalar(lnv[:, 0, b0:b1], mv[:, b0:b1, 1], EPS, None, ALU.add).then_inc(ln1_var, 1)

        def first_normed(b0, b1):
            link(dve.reciprocal(lnv[:, 2, b0:b1], lnv[:, 1, b0:b1]))
            for b in range(b0, b1):
                dve.tensor_scalar(xn[:, b, :], x[:, b, :], mv[:, b, 0:1], lnv[:, 2, b:b + 1], ALU.subtract,
                                  ALU.mult).then_inc(xn_done, 1)

        dve.wait_ge(x0_in, 16)
        first_norm(0, 1)
        dve.wait_ge(split_hi, 1)
        dve.tensor_tensor(kl[:, 0, 0:2, :], kt[:, 0, 0:2, :], kh[:, 0, 0:2, :], ALU.subtract).then_inc(lo_dve, 1)
        dve.wait_ge(roots, 1)
        first_normed(0, 1)
        dve.wait_ge(xn_done, 1)
        token_queries(0, 0)
        token_queries(0, 1)
        dve.wait_ge(x_in, 16)
        first_norm(1, B)
        take_queries(0, 0)
        dve.wait_ge(roots, 2)
        first_normed(1, B)
        for k in range(1, MT - 1):
            take_max(0, 0, k)
        shift(0, 0)
        take_shifted(0, 0)
        take_queries(0, 1)
        dve.wait_ge(xn_done, B)

        def body(i, off, total):
            more = exists(off, total, 1)
            if more:
                for k in range(1, 13):
                    take_max(i, off + 1, k)
                if exists(off, total, 2):
                    token_queries(i, off + 2)
                for k in range(13, MT - 1):
                    take_max(i, off + 1, k)
                shift(i, off + 1)
            if not (total and off == 0):
                invert(i, off - 1)
            if more:
                take_shifted(i, off + 1)
                if exists(off, total, 2):
                    take_queries(i, off + 2)
            if not (total and off == 0):
                divide(i, off - 1)

        def scale_win():
            dve.wait_ge(consts, NC)
            for c in range(C):
                dve.tensor_scalar(win[:, c, :], win[:, c, :], normw[:, c:c + 1], None, ALU.mult)\
                    .then_inc(win_done, 1)

        run_groups(dve, body, scale_win)
        invert(0, G - 1)
        divide(0, G - 1)

        dve.wait_ge(xb_done, B)
        for b in range(B):
            dve.wait_ge(proj_done, b + 1)
            dve.tensor_tensor(x1[:, b, :], bank[:, b, :], x[:, b, :], ALU.add).then_inc(x1_done, 1)
            dve.wait_ge(x1_done, b + 1)
            norm_stats(x1, b)
        dve.tensor_scalar(lnv[:, 0, :], mv[:, :, 1], EPS, None, ALU.add).then_inc(ln2_var, 1)
        dve.wait_ge(roots, 3)
        link(dve.reciprocal(lnv[:, 2, :], lnv[:, 1, :]))
        link(dve.tensor_tensor(lnv[:, 5, :], mv[:, :, 1], lnv[:, 2, :], ALU.mult))
        link(dve.tensor_tensor(lnv[:, 6, :], lnv[:, 5, :], lnv[:, 2, :], ALU.mult))
        dve.tensor_scalar(lnv[:, 3, :], lnv[:, 6, :], 1e-8, None, ALU.add).then_inc(ln2_ms, 1)
        dve.wait_ge(roots, 4)
        link(dve.reciprocal(lnv[:, 5, :], lnv[:, 4, :]))
        link(dve.tensor_tensor(lnv[:, 6, :], lnv[:, 5, :], lnv[:, 2, :], ALU.mult))
        for b in range(B):
            dve.tensor_scalar(hn[:, b, :], x1[:, b, :], mv[:, b, 0:1], lnv[:, 6, b:b + 1], ALU.subtract, ALU.mult)\
                .then_inc(hn_done, 1)
        for b in range(B):
            dve.tensor_scalar(xn[:, b, :], x1[:, b, :], mv[:, b, 0:1], lnv[:, 2, b:b + 1], ALU.subtract, ALU.mult)\
                .then_inc(h_done, 1)
        for b in range(1, B, 2):
            dve.wait_ge(hnT_ready, b + 1)
            dve.tensor_copy(hnT[:, :, b * P:(b + 1) * P], bank[:, 4 + b, :].rearrange("p (c n) -> p c n", c=C))\
                .then_inc(hnT_dve, 1)

        dve.wait_ge(dt_done, 1)
        link(dve.tensor_scalar(aa[:, :], dt_[:, :], -1.0, 1.0, ALU.mult, ALU.add))
        dve.wait_ge(ut_done, 1)
        link(dve.tensor_tensor(bb[:, :], dt_[:, :], ut[:, :], ALU.mult))
        for b in range(B):
            part = slice(b * P, (b + 1) * P)
            link(dve.tensor_tensor_scan(hsn[:, part], aa[:, part], bb[:, part], 0.0, ALU.mult, ALU.add))
        dve.wait_ge(sg_done, 1)
        dve.tensor_tensor(aa[:, :], hsn[:, :], sg[:, :], ALU.mult).then_inc(y_done, 1)
        for b in range(B):
            dve.wait_ge(scan_out, b + 1)
            dve.wait_ge(x2p_done, b + 1)
            dve.tensor_tensor(x2[:, b, :], bank[:, 4 + b, :], x2[:, b, :], ALU.add).then_inc(x2_done, 1)
            dve.wait_ge(x2_done, b + 1)
            norm_stats(x2, b)
        dve.tensor_scalar(lnv[:, 0, :], mv[:, :, 1], EPS, None, ALU.add).then_inc(ln3_var, 1)
        dve.wait_ge(roots, 5)
        link(dve.reciprocal(lnv[:, 2, :], lnv[:, 1, :]))
        for b in range(B):
            dve.tensor_scalar(xn[:, b, :], x2[:, b, :], mv[:, b, 0:1], lnv[:, 2, b:b + 1], ALU.subtract, ALU.mult)\
                .then_inc(h3_done, 1)

        link(dve.tensor_copy(gwh[:, :, 0:E], gwt[:, :, :]))
        dve.tensor_tensor(gwh[:, :, E:2 * E], gwt[:, :, :], gwh[:, :, 0:E], ALU.subtract).then_inc(gw_split, 1)
        for b in range(B):
            dve.wait_ge(xh_done, b + 1)
            dve.tensor_tensor(xl[:, :, b * P:(b + 1) * P], bank[:, b, :].rearrange("p (c n) -> p c n", c=C),
                              xh[:, :, b * P:(b + 1) * P], ALU.subtract).then_inc(xl_done, 1)
        dve.wait_ge(log_ready, 1)
        lg = bank[:, 4, 0:B * E].rearrange("p (b e) -> p b e", b=B)

        def over_e(col):
            return r1[:, col, :].unsqueeze(2).broadcast_to([P, B, E])

        link(dve.tensor_reduce(r1[:, 0, :], lg, AX.X, ALU.max))
        dve.tensor_tensor(lgs[:, 0, :, :], lg, over_e(0), ALU.subtract).then_inc(log_sub, 1)
        dve.wait_ge(log_exp, 1)
        link(dve.tensor_reduce(r1[:, 1, :], lgs[:, 1, :, :], AX.X, ALU.add))
        link(dve.reciprocal(r1[:, 2, :], r1[:, 1, :]))
        link(dve.tensor_tensor(lgs[:, 2, :, :], lgs[:, 1, :, :], over_e(2), ALU.mult))
        link(dve.tensor_tensor(lgs[:, 3, :, :], lgs[:, 2, :, :], gbias[:, :, :], ALU.add))
        for b in range(B):
            link(dve.max(top[:, b, :], lgs[:, 3, b, :]))
            link(dve.max_index(topi[:, b, :], top[:, b, :], lgs[:, 3, b, :]))
        link(dve.tensor_copy(topf[:, :, :], topi[:, :, :]))
        for b in range(B):
            link(dve.tensor_scalar(lgs[:, 4, b, :], iota[:, :], topf[:, b, 0:1], None, ALU.is_equal))
            link(dve.scalar_tensor_tensor(lgs[:, 5, b, :], iota[:, :], topf[:, b, 1:2], lgs[:, 4, b, :],
                                          ALU.is_equal, ALU.add))
        link(dve.tensor_tensor(lgs[:, 0, :, :], lgs[:, 5, :, :], lgs[:, 2, :, :], ALU.mult))
        link(dve.memset(g20[:, :, E:U], 1.0))
        link(dve.memset(g20[:, :, U + E:2 * U], 0.0))
        link(dve.tensor_copy(g20[:, :, 0:E], lgs[:, 0, :, :]))
        dve.tensor_tensor(g20[:, :, U:U + E], lgs[:, 0, :, :], g20[:, :, 0:E], ALU.subtract).then_inc(g20_done, 1)
        dve.wait_ge(gT_ready, 1)
        dve.tensor_copy(gT[:, :], half_bank(5)[0:2 * U, 0:T]).then_inc(gT_done, 1)
        for u in range(1, U, 2):
            dve.wait_ge(gate_ready, u + 1)
            dve.tensor_scalar(gate[:, u, :], bank[:, 4 + u % 4, :], 1.0 / WS, None, ALU.mult).then_inc(gate_dve, 1)

        def split_weights(i, off, m):
            n = m + 1 if isinstance(at(i, off), int) and off == 0 else 3 * at(i, off) + m + 1
            dve.wait_ge(w_hi, n)
            dve.scalar_tensor_tensor(wl[:, off % 2, m, :, :].rearrange("p c n -> p (c n)"),
                                     wst[:, off % 2, m, :, :].rearrange("p c n -> p (c n)"), WS,
                                     wh[:, off % 2, m, :, :].rearrange("p c n -> p (c n)"),
                                     ALU.mult, ALU.subtract).then_inc(w_lo, 1)

        for m in range(3):
            split_weights(0, 0, m)
        dve.wait_ge(gate_act, U // 2)
        dve.wait_ge(gate_dve, U // 2)

        def unit(i, off, total):
            for it in range(C):
                n = it if (total and off == 0) else C * at(i, off) + it
                dve.wait_ge(sil_done, n + 1)
                dve.tensor_tensor(hf[:, it % 2, :], bank[:, 5 + 2 * (it % 2), :], sil[:, it % 2, :], ALU.mult)\
                    .then_inc(mul_done, 1)
                dve.wait_ge(mul_done, n + 1)
                dve.tensor_tensor(hf[:, it % 2, :], hf[:, it % 2, :], gate[:, at(i, off), :], ALU.mult)\
                    .then_inc(h_full, 1)
                dve.wait_ge(h_hi, n + 1)
                if not (total and off == 0 and it < 2):
                    dve.wait_ge(down_done, n - 1)
                dve.tensor_tensor(hl[:, it % 2, :], hf[:, it % 2, :], hh[:, it % 2, :], ALU.subtract)\
                    .then_inc(h_lo, 1)
                if it < 3 and exists(off, total, 1):
                    split_weights(i, off + 1, it)

        run_units(dve, unit)
        dve.wait_ge(down_done, C * U)
        for b in range(B):
            dve.scalar_tensor_tensor(x1[:, b, :], bank[:, b, :], 1.0 / WS, x2[:, b, :], ALU.mult, ALU.add)\
                .then_inc(x3_done, 1)

    @blk.tensor
    def _(pe):
        def queries(i, off):
            pe.wait_ge(xs_step, 3 * at(i, off) + 3)
            if not (isinstance(at(i, off), int) and off == 0):
                pe.wait_ge(m_taken, MT * at(i, off) - 1)
            for a in range(HG):
                mm = pe.transpose(half_bank(4)[0:KS, a * P:(a + 1) * P], xs[:, off % 2, a, 0:KS], idh[:, :])
            mm.then_inc(m_ready, 1)

        def max_scores(i, off, k):
            a, q = block_of(k)
            if k == 1:
                pe.wait_ge(m_taken, MT * at(i, off) + 1)
            else:
                pe.wait_ge(m_taken, MT * at(i, off) + k - 1)
            if k % (2 * HG) == 1:
                pe.wait_ge(k_rep[off % 2][k // (2 * HG)], 16 * 6 * uses(i, off))
            pe.matmul(bank[:, 4 + k % 2, :], q1[:, a, :], kstk[0:KS, off % 2, a, q * 512:(q + 1) * 512],
                      start=True, stop=True).then_inc(m_ready, 1)

        def shifted(i, off):
            pe.wait_ge(mx_step, 3 * at(i, off) + 3)
            pe.wait_ge(m_taken, MT * at(i, off) + MT - 2)
            for a in range(HG):
                mm = pe.transpose(half_bank(5)[0:KM, a * P:(a + 1) * P], xs[:, off % 2, a, :], idh[:, :])
            mm.then_inc(m_ready, 1)

        def scores(i, off, hs, j):
            if hs == 0 and j == 0:
                pe.wait_ge(m_taken, MT * at(i, off) + MT)
            if j == 0 and not (isinstance(at(i, off), int) and off == 0 and hs < 2):
                pe.wait_ge(exp_done, HS * at(i, off) + hs - 1)
            tile = 2 * hs + j
            for a in range(HG):
                mm = pe.matmul(bank[:, 2 * (hs % 2) + j, a * P:(a + 1) * P],
                               kstk[:, off % 2, a, tile * P:(tile + 1) * P], q2[:, off % 2, a, :],
                               start=True, stop=True)
            if j == 1:
                mm.then_inc(st_done, 1)

        def values(i, off, hs, j):
            if j == 0:
                pe.wait_ge(exp_done, HS * at(i, off) + hs + 1)
            if hs == 0 and j == 0:
                pe.wait_ge(v_in[off % 2], 16 * uses(i, off))
                if not (isinstance(at(i, off), int) and off < 2):
                    pe.wait_ge(o_free, at(i, off - 1))
            tile = 2 * hs + j
            for a in range(HG):
                mm = pe.matmul(bank[a * HD:(a + 1) * HD, 6 + off % 2, 0:P], v[:, off % 2, tile, a * HD:(a + 1) * HD],
                               pt[:, hs % 4, j, a, :], start=(tile == 0), stop=(tile == J - 1),
                               skip_group_check=True)
            if j == 1:
                mm.then_inc(pv_done, 1)

        def denominators(i, off, hs):
            pe.wait_ge(add_done, HS * at(i, off) + hs + 1)
            for a in range(HG):
                mm = pe.matmul(bank[a * HD:(a + 1) * HD, 6 + off % 2, P:2 * P], ones[:, :], ps2[:, hs % 4, a, :],
                               start=False, stop=(hs == HS - 1), skip_group_check=True)
            mm.then_inc(den_done, 1)
            if hs == HS - 1:
                pe.wait_ge(den_done, HS * at(i, off) + HS)
                pe.nop().then_inc(o_ready, 1)

        pe.wait_ge(ones_set, 1)
        pe.wait_ge(id_in, 32)
        queries(0, 0)
        for k in range(1, MT - 1):
            max_scores(0, 0, k)
        shifted(0, 0)
        queries(0, 1)
        scores(0, 0, 0, 0)
        scores(0, 0, 0, 1)

        SPREAD = [(1, 2, 3), (4, 5, 6), (7, 8, 9), (10, 11, 12), (13, 14, 15), (16,)]

        def body(i, off, total):
            more = exists(off, total, 1)
            for hs in range(HS):
                tenants = list(SPREAD[hs]) if more and hs < len(SPREAD) else []

                def one_max():
                    if tenants:
                        max_scores(i, off + 1, tenants.pop(0))

                one_max()
                for j in range(2):
                    if hs + 1 < HS:
                        scores(i, off, hs + 1, j)
                    elif more:
                        scores(i, off + 1, 0, j)
                one_max()
                if hs == 7 and exists(off, total, 2):
                    queries(i, off + 2)
                values(i, off, hs, 0)
                if hs == 6 and more:
                    shifted(i, off + 1)
                values(i, off, hs, 1)
                one_max()
                if hs > 0:
                    denominators(i, off, hs - 1)
                elif not (total and off == 0):
                    denominators(i, off - 1, HS - 1)

        run_groups(pe, body)
        denominators(0, G - 1, HS - 1)

        pe.wait_ge(consts, NC)
        pe.wait_ge(o_free, G)
        for b in range(B):
            for c in range(C):
                mm = pe.matmul(bank[:, b, :], ao[:, C * b + c, :], wproj[:, c, :], start=(c == 0), stop=(c == C - 1))
            mm.then_inc(proj_done, 1)

        for b in range(B):
            pe.wait_ge(hn_done, b + 1)
            for c in range(C):
                mm = pe.transpose(bank[:, 4 + b, c * P:(c + 1) * P], hn[:, b, c * P:(c + 1) * P], idf[:, :])
            mm.then_inc(hnT_ready, 1)
        pe.wait_ge(hnT_act, B // 2)
        pe.wait_ge(hnT_dve, B // 2)
        pe.wait_ge(win_done, C)
        pe.wait_ge(x1_done, B)
        for c in range(C):
            mm = pe.matmul(bank[:, 0, :], win[:, c, 0:2 * ST], hnT[:, c, :], start=(c == 0), stop=(c == C - 1))
        mm.then_inc(uz_ready, 1)
        for c in range(C):
            mm = pe.matmul(bank[0:ST, 1, :], win[:, c, 2 * ST:3 * ST], hnT[:, c, :], start=(c == 0), stop=(c == C - 1))
        mm.then_inc(g_ready, 1)
        pe.wait_ge(uz_done, 1)
        pe.matmul(bank[0:ST, 2, :], wx[ST:2 * ST, :], uz[ST:2 * ST, :], start=True, stop=True).then_inc(dt_ready, 1)
        pe.matmul(bank[0:ST, 3, :], wx[0:ST, :], uz[0:ST, :], start=True, stop=True).then_inc(ut_ready, 1)
        pe.wait_ge(y_done, 1)
        for b in range(B):
            pe.matmul(bank[:, 4 + b, :], aa[:, b * P:(b + 1) * P], wout[:, :], start=True, stop=True)\
                .then_inc(scan_out, 1)

        for b in range(B):
            pe.wait_ge(h3_done, b + 1)
            for c in range(C):
                mm = pe.transpose(bank[:, b, c * P:(c + 1) * P], xn[:, b, c * P:(c + 1) * P], idf[:, :])
            mm.then_inc(h3T_ready, 1)
        pe.wait_ge(gw_split, 1)
        for b in range(B):
            part = slice(b * P, (b + 1) * P)
            pe.wait_ge(xl_done, b + 1)
            for c in range(C):
                pe.matmul(bank[:, 4, b * E:(b + 1) * E], xh[:, c, part], gwh[:, c, 0:E], start=(c == 0), stop=False)
                pe.matmul(bank[:, 4, b * E:(b + 1) * E], xh[:, c, part], gwh[:, c, E:2 * E], start=False, stop=False)
                mm = pe.matmul(bank[:, 4, b * E:(b + 1) * E], xl[:, c, part], gwh[:, c, 0:E], start=False,
                               stop=(c == C - 1))
        mm.then_inc(log_ready, 1)
        pe.wait_ge(zero_set, 1)
        for b in range(B):
            pe.matmul(bank[:, b, :], zero[:, 0:P], zero[:, :], start=True, stop=False, skip_group_check=True)
        pe.wait_ge(g20_done, 1)
        for b in range(B):
            mm = pe.transpose(half_bank(5)[0:2 * U, b * P:(b + 1) * P], g20[:, b, :], idh[:, :])
        mm.then_inc(gT_ready, 1)
        pe.wait_ge(gT_done, 1)
        for u in range(U):
            if u >= 4:
                pe.wait_ge((gate_act, gate_dve)[u % 2], (u - 4) // 2 + 1)
            pe.matmul(bank[:, 4 + u % 4, :], sel[:, u, :], gT[:, :], start=True, stop=True).then_inc(gate_ready, 1)
        pe.wait_ge(gate_act, U // 2)
        pe.wait_ge(gate_dve, U // 2)

        def up(i, off, it, n):
            part = slice(it * P, (it + 1) * P)
            q = off % 2
            for m in range(2):
                for c in range(C):
                    o = bank[:, 4 + 2 * (it % 2) + m, :]
                    pe.matmul(o, wh[:, q, m, c, part], xh[:, c, :], start=(c == 0), stop=False)
                    pe.matmul(o, wh[:, q, m, c, part], xl[:, c, :], start=False, stop=False)
                    mm = pe.matmul(o, wl[:, q, m, c, part], xh[:, c, :], start=False, stop=(c == C - 1))
            mm.then_inc(ab_ready, 1)

        def down(q, it, n):
            pe.wait_ge(h_hi, n)
            pe.wait_ge(h_lo, n)
            for b in range(B):
                part = slice(b * P, (b + 1) * P)
                pe.matmul(bank[:, b, :], hh[:, it % 2, part], wh[:, q, 2, it, :], start=False, stop=False,
                          skip_group_check=True)
                pe.matmul(bank[:, b, :], hh[:, it % 2, part], wl[:, q, 2, it, :], start=False, stop=False,
                          skip_group_check=True)
                mm = pe.matmul(bank[:, b, :], hl[:, it % 2, part], wh[:, q, 2, it, :], start=False, stop=False,
                               skip_group_check=True)
            mm.then_inc(down_done, 1)

        def unit(i, off, total):
            first = total and off == 0
            for it in range(C):
                n = it if first else C * at(i, off) + it
                if it == 0:
                    pe.wait_ge(w_hi, 3 * at(i, off) + 2)
                    pe.wait_ge(w_lo, 3 * at(i, off) + 2)
                if not (first and it < 2):
                    pe.wait_ge(mul_done, n - 1)
                up(i, off, it, n)
                if it == 0:
                    if not first:
                        down((off - 1) % 2, C - 1, n)
                else:
                    if it == 1:
                        pe.wait_ge(w_hi, 3 * at(i, off) + 3)
                        pe.wait_ge(w_lo, 3 * at(i, off) + 3)
                    down(off % 2, it - 1, n)

        run_units(pe, unit)
        down((U - 1) % 2, C - 1, C * U)

    block.__exit__(None, None, None)


def kernel(**inputs):
    import concourse.bacc as bacc
    from concourse.bass_utils import run_bass_kernel_spmd

    a = {k.replace("L0_", ""): np.asarray(v) for k, v in inputs.items()}
    ctx = a["ctx_1024"]
    def rows(w):
        w = w.reshape(*w.shape[:-2], w.shape[-2] // P, P, w.shape[-1])
        return np.moveaxis(w, -2, -3)

    def spread(row):
        return np.broadcast_to(row, (P, *row.shape))

    w1 = np.concatenate([a["ffn_w1"], a["ffn_sw1"].reshape(2, D, D)])
    w3 = np.concatenate([a["ffn_w3"], a["ffn_sw3"].reshape(2, D, D)])
    w2 = np.concatenate([a["ffn_w2"], a["ffn_sw2"].reshape(D, 2, D).transpose(1, 0, 2)])
    ffw = np.stack([rows(w.transpose(0, 2, 1)) for w in (w1, w3, w2)], axis=1)
    cols = np.zeros((P, 4), np.float32)
    cols[:, 0] = a["attn_b_in"][:P]
    cols[:ST, 1] = a["attn_b_in"][P:]
    cols[:ST, 2] = a["attn_b_x"]
    cols[:ST, 3] = a["attn_b_dt"]
    pick = np.concatenate([np.eye(U), np.eye(U)]).astype(np.float16)
    arrays = {
        "x": a["x"].transpose(1, 0, 2),
        "keysT": ctx.reshape(B, 4, S // 4, C, HG, HD).transpose(0, 3, 1, 5, 4, 2).reshape(G, P, HG, S // 4),
        "vals": ctx.reshape(B, J, P, C, P).transpose(0, 3, 2, 1, 4).reshape(G, P, J, P),
        "ffw": ffw,
        "wproj": rows(a["xattn_w_proj"].T),
        "win": rows(a["attn_W_in"]),
        "normw": a["attn_norm_w"].reshape(C, P).T,
        "bproj": spread(a["xattn_b_proj"]),
        "bout": spread(a["attn_b_out"]),
        "wx": np.concatenate([a["attn_W_x"], a["attn_W_dt"]]),
        "wout": a["attn_W_out"],
        "cols": cols,
        "gwt": rows(a["ffn_gate_w"].T),
        "gbias": spread(np.broadcast_to(a["ffn_gate_bias"], (B, E))),
        "iota": spread(np.arange(E, dtype=np.float32)),
        "idf": np.eye(P, dtype=np.float32),
        "idh": np.eye(P, dtype=np.float16),
        "ones": np.ones((KM - KS, 2, HG, S), np.float16),
        "sel": np.broadcast_to(pick[:, :, None], (2 * U, U, P)),
    }
    nc = bacc.Bacc("TRN2", target_bir_lowering=False, num_devices=1)
    feed, aps = {}, {}
    for name, arr in arrays.items():
        arr = np.ascontiguousarray(arr)
        feed[f"in_{name}"] = arr
        aps[name] = nc.dram_tensor(f"in_{name}", arr.shape, mybir.dt.from_np(arr.dtype), kind="ExternalInput").ap()
    out = nc.dram_tensor("out_0", (B, P, D), F32, kind="ExternalOutput").ap()
    build_program(nc, aps, out)
    r = run_bass_kernel_spmd(nc, [feed], core_ids=[0])
    return r.results[0]["out_0"]
```

```python
import concourse.bass as bass
from concourse import mybir
import numpy as np

F32 = mybir.dt.float32
F16 = mybir.dt.float16
U32 = mybir.dt.uint32
ALU = mybir.AluOpType
ACT = mybir.ActivationFunctionType
AX = mybir.AxisListType

P = 128
B = 4
D = 512
C = D // P
S = 2048
J = S // P
HD = 32
HG = P // HD
G = B * C
T = B * P
ST = 64
E = 8
U = 2 + E
HS = J // 2
MT = 2 + HG * HG
KS = 3 * HD
KM = KS + 2
SC = float(HD) ** -0.5
EPS = 1e-5
WS = 16.0


def build_program(nc, t, out):
    sb = nc.alloc_sbuf_tensor
    scoped = []

    def temp(name, shape, dt):
        h = nc.sbuf_tensor(name, shape, dt)
        scoped.append(h)
        return h.__enter__()

    x = sb("x_tok", [P, B, D], F32)
    xn = sb("xn", [P, B, D], F32)
    ao = sb("ao", [P, G, P], F32)
    wproj = sb("wproj", [P, C, D], F32)
    win = sb("win", [P, C, 4 * ST], F32)
    normw = sb("normw", [P, C], F32)
    bproj = sb("bproj", [P, D], F32)
    bout = sb("bout", [P, D], F32)
    wx = sb("wx", [P, 2 * ST], F32)
    wout = sb("wout", [P, D], F32)
    cols = sb("cols", [P, 4], F32)
    eps = sb("eps", [P, 2], F32)
    gwt = sb("gwt", [P, C, E], F32)
    gbias = sb("gbias", [P, B, E], F32)
    iota = sb("iota", [P, E], F32)
    idf = sb("idf", [P, P], F32)
    idh = sb("idh", [P, P], F16)
    wst = sb("wst", [P, 2, 3, C, D], F32)
    zero = sb("zero", [P, 512], F16)
    mv = sb("mv", [P, B, 2], F32)
    st6 = sb("st6", [P, B, 6], F32)
    lnv = sb("lnv", [P, 4, B], F32)

    gwh = sb("gwh", [P, C, 2 * E], F16)
    lgs = sb("lgs", [P, 6, B, E], F32)
    top = sb("top", [P, B, 8], F32)
    topi = sb("topi", [P, B, 8], U32)
    topf = sb("topf", [P, B, 8], F32)
    gT = sb("gT", [E, T], F32)
    r1 = sb("r1", [P, 3, B], F32)

    kt = temp("kt", [P, 2, HG, S // 4], F32)
    kh = temp("kh", [P, 2, HG, S // 4], F16)
    kl = temp("kl", [P, 2, HG, S // 4], F16)
    kstk = temp("kstk", [KM, 2, HG, S], F16)
    v = temp("v", [P, 2, J, P], F32)
    pt = temp("pt", [P, 4, 2, HG, P], F32)
    ps2 = temp("ps2", [P, 4, HG, P], F32)
    xs = temp("xs", [P, 2, HG, KM], F16)
    q1 = temp("q1", [KS, HG, P], F16)
    q2 = temp("q2", [KM, 2, HG, P], F16)
    mx = temp("mx", [P, HG, HG], F32)
    negm = temp("negm", [P, HG], F32)
    rden = temp("rden", [P, P], F32)
    ones = temp("ones", [P, HD], F32)
    for h in reversed(scoped):
        h.__exit__(None, None, None)
    scoped.clear()

    ws = temp("ws", [P, 2, 2, 3, C, D], F16)
    gate = temp("gate", [P, U, T], F32)
    xh = temp("xh", [P, C, T], F16)
    xl = temp("xl", [P, C, T], F16)
    sil = temp("sil", [P, 2, T], F32)
    hf = temp("hf", [P, 2, T], F32)
    hh = temp("hh", [P, 2, T], F16)
    hl = temp("hl", [P, 2, T], F16)
    x1 = temp("x1", [P, B, D], F32)
    x2 = temp("x2", [P, B, D], F32)
    for h in reversed(scoped):
        h.__exit__(None, None, None)
    scoped.clear()
    temp("first_slot", [P, 2 * 3 * C * D], F16)
    hn = temp("scan_hn", [P, B, D], F32)
    hnT = temp("scan_hnT", [P, C, T], F32)
    uz = temp("scan_uz", [P, T], F32)
    sg = temp("scan_sg", [P, T], F32)
    ut = temp("scan_ut", [P, T], F32)
    dt_ = temp("scan_dt", [P, T], F32)
    aa = temp("scan_a", [P, T], F32)
    bb = temp("scan_b", [P, T], F32)
    hsn = temp("scan_h", [P, T], F32)
    yst = temp("scan_y", [P, T], F16)
    wo = temp("scan_wo", [P, 2, D], F16)
    for h in reversed(scoped):
        h.__exit__(None, None, None)
    scoped.clear()
    gates = nc.dram_tensor("gates", (E, T), F32, kind="Internal").ap()
    bank = nc.alloc_psum_tensor("bank", [P, 8, 512], F32)

    def half_bank(n):
        return bank[:, n, :].bitcast(F16)

    sem = nc.alloc_semaphore
    consts = sem("consts_loaded")
    x_in = sem("x_loaded")
    x0_in = sem("x_first_batch_loaded")
    id_in = sem("identity_and_ones_loaded")
    kt_in = [sem("kt_loaded_0"), sem("kt_loaded_1")]
    v_in = [sem("v_loaded_0"), sem("v_loaded_1")]
    k_rep = [[sem(f"k_stacked_{q}_{h}") for h in range(2)] for q in range(2)]
    split_hi = sem("split_hi")
    split_lo = sem("split_lo")
    lo_dve = sem("split_lo_by_vector")
    ones_set = sem("ones_set")
    zero_set = sem("zero_set")
    chain = sem("vector_chain")
    ln1_var = sem("ln1_var")
    roots = sem("roots")
    xn_done = sem("xn_done")
    xb_done = sem("x_plus_b_proj")
    win_done = sem("win_scaled")
    xs_step = sem("xs_step")
    m_ready = sem("max_ring_filled")
    m_taken = sem("max_ring_taken")
    mx_step = sem("max_step")
    st_done = sem("scores_ready")
    exp_done = sem("exp_done")
    add_done = sem("pair_sums_ready")
    pv_done = sem("pv_done")
    den_done = sem("den_done")
    o_ready = sem("o_ready")
    o_rd = sem("o_reciprocal")
    o_free = sem("o_taken")
    proj_done = sem("proj_done")
    x1_done = sem("x1_done")
    ln2_var = sem("ln2_var")
    hn_done = sem("hn_done")
    h_done = sem("h_done")
    x1b_done = sem("x1_plus_b_out")
    x2p_done = sem("x2_residual")
    hnT_ready = sem("hnT_ready")
    hnT_act = sem("hnT_copied_scalar")
    uz_ready = sem("uz_ready")
    g_ready = sem("g_ready")
    uz_done = sem("uz_copied")
    sg_done = sem("sg_done")
    dt_ready = sem("dt_ready")
    ut_ready = sem("ut_ready")
    dt_done = sem("dt_done")
    ut_done = sem("ut_done")
    y_done = sem("y_done")
    scan_out = sem("scan_out_ready")
    x2_done = sem("x2_done")
    ln3_var = sem("ln3_var")
    h3_done = sem("h3_done")
    h3T_ready = sem("h3T_ready")
    xh_done = sem("xh_done")
    xl_done = sem("xl_done")
    gw_split = sem("router_weights_split")
    log_ready = sem("logits_ready")
    log_sub = sem("logits_minus_max")
    log_exp = sem("logits_exp")
    w_in = [[sem(f"w{m}_loaded_{q}") for m in range(3)] for q in range(2)]
    g_made = sem("gates_made")
    gT_ready = sem("gates_transposed")
    gT_done = sem("gates_transposed_copied")
    g_stored = sem("gates_stored")
    g_spread = sem("gates_spread")
    one_gate = sem("shared_gates_set")
    eps_set = sem("eps_set")
    wo_hi = sem("w_out_high")
    wo_lo = sem("w_out_low")
    w_hi = sem("w_hi")
    w_lo = sem("w_lo")
    ab_ready = sem("up_ready")
    sil_done = sem("silu_done")
    mul_done = sem("mul_done")
    h_full = sem("h_full")
    h_hi = sem("h_hi")
    h_lo = sem("h_lo")
    down_done = sem("down_done")
    y_ready = sem("mixture_ready")
    x3_done = sem("x3_done")
    stored = sem("stored")

    def at(i, off):
        return 2 * i + off

    def uses(i, off):
        return i + off // 2 + 1

    def run_groups(eng, body, before_last=None):
        body(0, 0, G)
        with eng.Fori(0, (G - 4) // 2) as i:
            body(i, 1, None)
            body(i, 2, None)
        body(0, G - 3, G)
        body(0, G - 2, G)
        if before_last:
            before_last()
        body(0, G - 1, G)

    def run_units(eng, body):
        body(0, 0, U)
        with eng.Fori(0, (U - 2) // 2) as i:
            body(i, 1, None)
            body(i, 2, None)
        body(0, U - 1, U)

    def exists(off, total, ahead):
        return total is None or off + ahead < total

    def block_of(k):
        h, k = divmod(k - 1, 2 * HG)
        return k // 2, 2 * h + k % 2

    CONSTS = [(wproj[:, :, :], "wproj"), (win[:, :, :], "win"), (normw[:, :], "normw"), (bproj[:, :], "bproj"),
              (bout[:, :], "bout"), (wx[:, :], "wx"), (wout[:, :], "wout"), (cols[:, :], "cols"),
              (gwt[:, :, :], "gwt"), (gbias[:, :, :], "gbias"), (iota[:, :], "iota"), (idf[:, :], "idf")]

    block = nc.Block()
    blk = block.__enter__()

    @blk.sync
    def _(sp):
        def load_k(i, off):
            sp.dma_start(kt[:, off % 2, :, :], t["keysT"][at(i, off)]).then_inc(kt_in[off % 2], 16)

        def load_v(i, off):
            sp.dma_start(v[:, off % 2, :, :], t["vals"][at(i, off)]).then_inc(v_in[off % 2], 16)

        def copies(off, h, src, rows):
            for row in rows:
                for q in (2 * h, 2 * h + 1):
                    sp.dma_start(kstk[row:row + HD, off % 2, :, q * S // 4:(q + 1) * S // 4],
                                 src[q * HD:(q + 1) * HD, off % 2, :, :]).then_inc(k_rep[off % 2][h], 16)

        def stack(off, h):
            copies(off, h, kh, (0, 2 * HD))
            copies(off, h, kl, (HD,))

        sp.dma_start(x[:, 0, :], t["x"][:, 0, :]).then_inc(x0_in, 16)
        load_k(0, 0)
        sp.dma_start(idh[:, :], t["idh"]).then_inc(id_in, 16)
        sp.dma_start(kstk[KS:KM, :, :, :], t["ones"]).then_inc(id_in, 16)
        sp.dma_start(x[:, 1:B, :], t["x"][:, 1:B, :]).then_inc(x_in, 16)
        load_k(0, 1)
        sp.wait_ge(split_hi, 2)
        copies(0, 0, kh, (0, 2 * HD))
        sp.wait_ge(lo_dve, 1)
        sp.wait_ge(split_lo, 1)
        copies(0, 0, kl, (HD,))
        stack(0, 1)
        load_v(0, 0)
        sp.wait_ge(split_lo, 2)
        stack(1, 0)
        load_k(0, 2)
        stack(1, 1)

        def body(i, off, total):
            if exists(off, total, 3):
                sp.wait_ge(split_lo, at(i, off + 2))
                load_k(i, off + 3)
            if exists(off, total, 1):
                if off > 0 or total is None:
                    sp.wait_ge(pv_done, HS * at(i, off))
                load_v(i, off + 1)
            if exists(off, total, 2):
                sp.wait_ge(st_done, HS * at(i, off) + HS // 2)
                sp.wait_ge(split_lo, at(i, off + 3))
                stack(off + 2, 0)
                sp.wait_ge(st_done, HS * at(i, off + 1))
                stack(off + 2, 1)

        body(0, 0, G)
        with sp.Fori(0, (G - 4) // 2) as i:
            body(i, 1, None)
            body(i, 2, None)
        body(0, G - 3, G)
        for dst, name in CONSTS:
            sp.dma_start(dst, t[name]).then_inc(consts, 16)
        body(0, G - 2, G)
        for u in range(2):
            for m in range(3):
                sp.dma_start(wst[:, u, m, :, :], t["ffw"][u, m]).then_inc(w_in[u][m], 16)
        body(0, G - 1, G)

        def load_w(i, off):
            sp.wait_ge(w_lo, 3 * at(i, off - 1))
            for m in range(3):
                sp.dma_start(wst[:, off % 2, m, :, :], t["ffw"][at(i, off), m]).then_inc(w_in[off % 2][m], 16)

        sp.wait_ge(gT_done, 1)
        sp.dma_start(gates, gT[:, :]).then_inc(g_stored, 16)
        sp.wait_ge(g_stored, 16)
        sp.dma_start(gate[:, 2:U, :].rearrange("p e t -> p (e t)"),
                     gates.rearrange("e t -> (e t)").partition_broadcast(P)).then_inc(g_spread, 16)
        with sp.Fori(0, (U - 2) // 2) as i:
            load_w(i, 2)
            load_w(i, 3)
        for b in range(B):
            sp.wait_ge(x3_done, b + 1)
            sp.dma_start(out[b], x1[:, b, :]).then_inc(stored, 16)
        sp.wait_ge(stored, 16 * B)

    NC = 16 * len(CONSTS)

    @blk.scalar
    def _(act):
        def split_keys(i, off, h):
            heads = slice(h * HG // 2, (h + 1) * HG // 2)
            if h == 0:
                act.wait_ge(kt_in[off % 2], 16 * uses(i, off))
            act.activation(kh[:, off % 2, heads, :].rearrange("p a s -> p (a s)"),
                           kt[:, off % 2, heads, :].rearrange("p a s -> p (a s)"), ACT.Copy).then_inc(split_hi, 1)

        def root(ready, count, b0, b1):
            act.wait_ge(ready, count)
            act.activation(lnv[:, 0, b0:b1], mv[:, b0:b1, 1], ACT.Sqrt, bias=eps[:, 0:1]).then_inc(roots, 1)

        for h in range(2):
            split_keys(0, 0, h)
        act.wait_ge(eps_set, 2)
        root(ln1_var, 1, 0, 1)
        for h in range(2):
            split_keys(0, 1, h)
        root(ln1_var, B, 1, B)
        for h in range(2):
            act.wait_ge(k_rep[0][h], 16 * 6)
        for h in range(2):
            split_keys(0, 2, h)

        def body(i, off, total):
            for hs in range(HS):
                act.wait_ge(st_done, HS * at(i, off) + hs + 1)
                if not (total and off == 0 and hs < 4):
                    act.wait_ge(pv_done, HS * at(i, off) + hs - 3)
                    act.wait_ge(add_done, HS * at(i, off) + hs - 3)
                act.activation(pt[:, hs % 4, :, :, :].rearrange("p j a t -> p (j a t)"),
                               bank[:, 2 * (hs % 2):2 * (hs % 2) + 2, :].rearrange("p j n -> p (j n)"),
                               ACT.Exp, scale=SC).then_inc(exp_done, 1)
                if hs in (3, 4) and exists(off, total, 3):
                    if hs == 3:
                        for h in range(2):
                            act.wait_ge(k_rep[(off + 1) % 2][h], 16 * 6 * uses(i, off + 1))
                    split_keys(i, off + 3, hs - 3)

        run_groups(act, body)

        def split_weights(i, off, m):
            act.wait_ge(w_in[off % 2][m], 16 * uses(i, off))
            act.activation(ws[:, off % 2, 0, m, :, :].rearrange("p c n -> p (c n)"),
                           wst[:, off % 2, m, :, :].rearrange("p c n -> p (c n)"), ACT.Copy, scale=WS)\
                .then_inc(w_hi, 1)

        def copy_high(b):
            act.wait_ge(h3T_ready, b + 1)
            act.activation(xh[:, :, b * P:(b + 1) * P], bank[:, b, :].rearrange("p (c n) -> p c n", c=C),
                           ACT.Copy).then_inc(xh_done, 1)

        def copy_normed(b):
            act.wait_ge(hnT_ready, b + 1)
            act.activation(hnT[:, :, b * P:(b + 1) * P], bank[:, 4 + b, :].rearrange("p (c n) -> p c n", c=C),
                           ACT.Copy).then_inc(hnT_act, 1)

        for b in range(B):
            root(ln2_var, b + 1, b, b + 1)
            act.activation(lnv[:, 1, b:b + 1], mv[:, b:b + 1, 1], ACT.Sqrt, bias=eps[:, 1:2],
                           scale=1.0 + 1e-8).then_inc(roots, 1)
            if b == 0:
                act.wait_ge(x1_done, 1)
                split_weights(0, 0, 0)
            else:
                copy_normed(b - 1)
        act.wait_ge(consts, NC)
        act.activation(wo[:, 0, :], wout[:, :], ACT.Copy, scale=WS).then_inc(wo_hi, 1)
        copy_normed(B - 1)
        split_weights(0, 0, 1)
        act.wait_ge(uz_ready, 2)
        act.activation(uz[:, :], bank[:, 0, :], ACT.Identity, bias=cols[:, 0:1]).then_inc(uz_done, 1)
        act.wait_ge(dt_ready, 1)
        act.activation(dt_[:, :], bank[:, 2, :], ACT.Sigmoid, bias=cols[:, 3:4]).then_inc(dt_done, 1)
        act.wait_ge(ut_ready, 1)
        act.activation(ut[:, :], bank[:, 3, :], ACT.Tanh, bias=cols[:, 2:3]).then_inc(ut_done, 1)
        act.wait_ge(g_ready, 3)
        act.activation(sg[:, :], bank[:, 1, :], ACT.Sigmoid, bias=cols[:, 1:2]).then_inc(sg_done, 1)
        split_weights(0, 0, 2)
        for b in range(B):
            root(ln3_var, b + 1, b, b + 1)
            if b > 0:
                copy_high(b - 1)
        copy_high(B - 1)

        act.wait_ge(log_sub, 1)
        act.activation(lgs[:, 1, :, :], lgs[:, 0, :, :], ACT.Exp).then_inc(log_exp, 1)

        def unit(i, off, total):
            for it in range(C):
                n = it if (total and off == 0) else C * at(i, off) + it
                act.wait_ge(ab_ready, n + 1)
                if not (total and off == 0 and it < 2):
                    act.wait_ge(mul_done, n - 1)
                act.activation(sil[:, it % 2, :], bank[:, 4 + 2 * (it % 2), :], ACT.Silu, scale=1.0 / WS)\
                    .then_inc(sil_done, 1)
                act.wait_ge(h_full, n + 1)
                if not (total and off == 0 and it < 2):
                    act.wait_ge(down_done, n - 1)
                act.activation(hh[:, it % 2, :], hf[:, it % 2, :], ACT.Copy).then_inc(h_hi, 1)
                if it < 3 and exists(off, total, 1):
                    if it == 0 and not (total and off == 0):
                        act.wait_ge(down_done, n)
                    split_weights(i, off + 1, it)

        run_units(act, unit)

    @blk.gpsimd
    def _(pool):
        def split_keys(i, off, a):
            if a % 2 == 0:
                pool.wait_ge(split_hi, 2 * at(i, off) + a // 2 + 1)
            low = pool.tensor_tensor(kl[:, off % 2, a, :], kt[:, off % 2, a, :], kh[:, off % 2, a, :], ALU.subtract)
            if a == HG - 1:
                low.then_inc(split_lo, 1)

        pool.memset(ones[:, :], 1.0).then_inc(ones_set, 1)
        pool.memset(zero[:, :], 0.0).then_inc(zero_set, 1)
        pool.memset(eps[:, 0:1], EPS).then_inc(eps_set, 1)
        pool.memset(eps[:, 1:2], EPS * 1e-8).then_inc(eps_set, 1)
        for a in range(2, HG):
            split_keys(0, 0, a)
        for n in range(1, 3):
            for a in range(HG):
                split_keys(0, n, a)

        def body(i, off, total):
            for hs in range(HS):
                pool.wait_ge(exp_done, HS * at(i, off) + hs + 1)
                if not (total and off == 0 and hs < 4):
                    pool.wait_ge(den_done, HS * at(i, off) + hs - 3)
                pool.tensor_tensor(ps2[:, hs % 4, :, :], pt[:, hs % 4, 0, :, :], pt[:, hs % 4, 1, :, :], ALU.add)\
                    .then_inc(add_done, 1)
                if hs in (1, 3) and exists(off, total, 2) and not (total and off == 0):
                    split_keys(i, off + 2, 2 + hs // 2)
                if hs in (5, 7) and exists(off, total, 3):
                    split_keys(i, off + 3, hs // 2 - 2)

        def add_bias():
            pool.wait_ge(xn_done, B)
            pool.wait_ge(consts, NC)
            for b in range(B):
                pool.tensor_tensor(x[:, b, :], x[:, b, :], bproj[:, :], ALU.add).then_inc(xb_done, 1)

        run_groups(pool, body)
        add_bias()
        for b in range(B):
            pool.wait_ge(x1_done, b + 1)
            pool.tensor_tensor(x2[:, b, :], x1[:, b, :], bout[:, :], ALU.add).then_inc(x1b_done, 1)
        for b in range(B):
            pool.wait_ge(h_done, b + 1)
            pool.wait_ge(x1b_done, b + 1)
            pool.tensor_tensor(x2[:, b, :], x2[:, b, :], xn[:, b, :], ALU.add).then_inc(x2p_done, 1)
        pool.wait_ge(scan_out, B)
        pool.memset(gate[:, 0:2, :], 1.0 / WS).then_inc(one_gate, 1)

    @blk.vector
    def _(dve):
        links = [0]

        def link(ins):
            links[0] += 1
            ins.then_inc(chain, 1)
            dve.wait_ge(chain, links[0])

        def stats(src, b, done):
            link(dve.bn_stats(st6[:, b, :], src[:, b, :]))
            dve.bn_aggr(mv[:, b, :], st6[:, b, :]).then_inc(done, 1)

        def token_queries(i, off):
            q = xn[:, :, :].rearrange("p b (c n) -> p (b c) n", c=C)[:, at(i, off), :]\
                .rearrange("p (a d) -> p a d", a=HG)
            z = xs[:, off % 2, :, :]
            dve.tensor_copy(z[:, :, 0:HD], q).then_inc(xs_step, 1)
            dve.tensor_copy(z[:, :, HD:2 * HD], q).then_inc(xs_step, 1)
            dve.wait_ge(xs_step, 3 * at(i, off) + 1)
            dve.tensor_tensor(z[:, :, 2 * HD:KS], q, z[:, :, 0:HD], ALU.subtract).then_inc(xs_step, 1)

        def take_queries(i, off):
            dve.wait_ge(m_ready, MT * at(i, off) + 1)
            dve.tensor_copy(q1[:, :, :], half_bank(4)[0:KS, 0:512].rearrange("k (a t) -> k a t", a=HG))\
                .then_inc(m_taken, 1)

        def take_max(i, off, k):
            a, q = block_of(k)
            dve.wait_ge(m_ready, MT * at(i, off) + k + 1)
            dve.tensor_reduce(mx[:, a, q:q + 1], bank[:, 4 + k % 2, :], AX.X, ALU.max).then_inc(m_taken, 1)

        def shift(i, off):
            dve.wait_ge(m_taken, MT * at(i, off) + MT - 1)
            dve.tensor_reduce(negm[:, :], mx[:, :, :], AX.X, ALU.max, negate=True).then_inc(mx_step, 1)
            dve.wait_ge(mx_step, 3 * at(i, off) + 1)
            z = xs[:, off % 2, :, :]
            dve.tensor_copy(z[:, :, KS:KS + 1], negm[:, :].unsqueeze(2)).then_inc(mx_step, 1)
            dve.wait_ge(mx_step, 3 * at(i, off) + 2)
            dve.tensor_tensor(z[:, :, KS + 1:KM], negm[:, :].unsqueeze(2), z[:, :, KS:KS + 1], ALU.subtract)\
                .then_inc(mx_step, 1)

        def take_shifted(i, off):
            dve.wait_ge(m_ready, MT * at(i, off) + MT)
            if not isinstance(at(i, off), int) or off >= 2:
                dve.wait_ge(st_done, HS * at(i, off - 1))
            dve.tensor_copy(q2[:, off % 2, :, :], half_bank(5)[0:KM, 0:512].rearrange("k (a t) -> k a t", a=HG))\
                .then_inc(m_taken, 1)

        def invert(i, off):
            dve.wait_ge(o_ready, at(i, off) + 1)
            if not (isinstance(at(i, off), int) and off == 0):
                dve.wait_ge(o_free, at(i, off))
            dve.reciprocal(rden[:, :], bank[:, 6 + off % 2, P:2 * P]).then_inc(o_rd, 1)

        def divide(i, off):
            dve.wait_ge(o_rd, at(i, off) + 1)
            dve.tensor_tensor(ao[:, at(i, off), :], bank[:, 6 + off % 2, 0:P], rden[:, :], ALU.mult)\
                .then_inc(o_free, 1)

        def first_norm(b0, b1):
            for b in range(b0, b1):
                stats(x, b, ln1_var)

        def first_normed(b0, b1):
            link(dve.reciprocal(lnv[:, 2, b0:b1], lnv[:, 0, b0:b1]))
            for b in range(b0, b1):
                dve.tensor_scalar(xn[:, b, :], x[:, b, :], mv[:, b, 0:1], lnv[:, 2, b:b + 1], ALU.subtract,
                                  ALU.mult).then_inc(xn_done, 1)

        dve.wait_ge(x0_in, 16)
        first_norm(0, 1)
        dve.wait_ge(split_hi, 1)
        dve.tensor_tensor(kl[:, 0, 0:2, :], kt[:, 0, 0:2, :], kh[:, 0, 0:2, :], ALU.subtract).then_inc(lo_dve, 1)
        dve.wait_ge(roots, 1)
        first_normed(0, 1)
        dve.wait_ge(xn_done, 1)
        token_queries(0, 0)
        token_queries(0, 1)
        dve.wait_ge(x_in, 16)
        first_norm(1, B)
        take_queries(0, 0)
        for k in range(1, MT - 1):
            take_max(0, 0, k)
        shift(0, 0)
        take_shifted(0, 0)
        take_queries(0, 1)
        dve.wait_ge(roots, 2)
        first_normed(1, B)
        dve.wait_ge(xn_done, B)

        def body(i, off, total):
            more = exists(off, total, 1)
            if more:
                for k in range(1, 13):
                    take_max(i, off + 1, k)
                if exists(off, total, 2):
                    token_queries(i, off + 2)
                for k in range(13, MT - 1):
                    take_max(i, off + 1, k)
                shift(i, off + 1)
            if not (total and off == 0):
                invert(i, off - 1)
            if more:
                take_shifted(i, off + 1)
            if not (total and off == 0):
                divide(i, off - 1)
            if exists(off, total, 2):
                take_queries(i, off + 2)

        def scale_win():
            dve.wait_ge(consts, NC)
            for c in range(C):
                dve.tensor_scalar(win[:, c, :], win[:, c, :], normw[:, c:c + 1], None, ALU.mult)\
                    .then_inc(win_done, 1)

        run_groups(dve, body, scale_win)
        invert(0, G - 1)
        divide(0, G - 1)

        def split_weights(i, off, m):
            n = m + 1 if isinstance(at(i, off), int) and off == 0 else 3 * at(i, off) + m + 1
            dve.wait_ge(w_hi, n)
            dve.scalar_tensor_tensor(ws[:, off % 2, 1, m, :, :].rearrange("p c n -> p (c n)"),
                                     wst[:, off % 2, m, :, :].rearrange("p c n -> p (c n)"), WS,
                                     ws[:, off % 2, 0, m, :, :].rearrange("p c n -> p (c n)"),
                                     ALU.mult, ALU.subtract).then_inc(w_lo, 1)

        dve.wait_ge(xb_done, B)
        for b in range(B):
            dve.wait_ge(proj_done, b + 1)
            dve.tensor_tensor(x1[:, b, :], bank[:, b, :], x[:, b, :], ALU.add).then_inc(x1_done, 1)
            dve.wait_ge(x1_done, b + 1)
            stats(x1, b, ln2_var)
            dve.wait_ge(roots, 4 + 2 * b)
            link(dve.reciprocal(lnv[:, 2:4, b:b + 1], lnv[:, 0:2, b:b + 1]))
            dve.tensor_scalar(hn[:, b, :], x1[:, b, :], mv[:, b, 0:1], lnv[:, 3, b:b + 1], ALU.subtract, ALU.mult)\
                .then_inc(hn_done, 1)
            dve.tensor_scalar(xn[:, b, :], x1[:, b, :], mv[:, b, 0:1], lnv[:, 2, b:b + 1], ALU.subtract, ALU.mult)\
                .then_inc(h_done, 1)
        dve.wait_ge(wo_hi, 1)
        dve.scalar_tensor_tensor(wo[:, 1, :], wout[:, :], WS, wo[:, 0, :], ALU.mult, ALU.subtract).then_inc(wo_lo, 1)
        link(dve.tensor_copy(gwh[:, :, 0:E], gwt[:, :, :]))
        dve.tensor_tensor(gwh[:, :, E:2 * E], gwt[:, :, :], gwh[:, :, 0:E], ALU.subtract).then_inc(gw_split, 1)
        split_weights(0, 0, 0)
        split_weights(0, 0, 1)

        dve.wait_ge(dt_done, 1)
        link(dve.tensor_scalar(aa[:, :], dt_[:, :], -1.0, 1.0, ALU.mult, ALU.add))
        dve.wait_ge(ut_done, 1)
        link(dve.tensor_tensor(bb[:, :], dt_[:, :], ut[:, :], ALU.mult))
        for b in range(B):
            part = slice(b * P, (b + 1) * P)
            scan = dve.tensor_tensor_scan(hsn[:, part], aa[:, part], bb[:, part], 0.0, ALU.mult, ALU.add)
        link(scan)
        dve.wait_ge(sg_done, 1)
        for n in range(2):
            part = slice(n * T // 2, (n + 1) * T // 2)
            dve.tensor_tensor(yst[:, part], hsn[:, part], sg[:, part], ALU.mult)
            link(dve.tensor_tensor(aa[:, part], hsn[:, part], sg[:, part], ALU.mult))
            dve.tensor_tensor(yst[ST:2 * ST, part], aa[ST:2 * ST, part], yst[ST:2 * ST, part], ALU.subtract)\
                .then_inc(y_done, 1)

        def third_norm(b):
            dve.wait_ge(roots, 11 + b)
            link(dve.reciprocal(lnv[:, 2, b:b + 1], lnv[:, 0, b:b + 1]))
            dve.tensor_scalar(xn[:, b, :], x2[:, b, :], mv[:, b, 0:1], lnv[:, 2, b:b + 1], ALU.subtract,
                              ALU.mult).then_inc(h3_done, 1)

        def split_tokens(b):
            dve.wait_ge(xh_done, b + 1)
            dve.tensor_tensor(xl[:, :, b * P:(b + 1) * P], bank[:, b, :].rearrange("p (c n) -> p c n", c=C),
                              xh[:, :, b * P:(b + 1) * P], ALU.subtract).then_inc(xl_done, 1)

        for b in range(B):
            dve.wait_ge(scan_out, b + 1)
            dve.wait_ge(x2p_done, b + 1)
            dve.scalar_tensor_tensor(x2[:, b, :], bank[:, 4 + b, :], 1.0 / WS, x2[:, b, :], ALU.mult, ALU.add)\
                .then_inc(x2_done, 1)
            dve.wait_ge(x2_done, b + 1)
            stats(x2, b, ln3_var)
            if b > 0:
                third_norm(b - 1)
            if b > 1:
                split_tokens(b - 2)
        third_norm(B - 1)
        split_tokens(B - 2)
        split_tokens(B - 1)
        split_weights(0, 0, 2)

        dve.wait_ge(log_ready, 1)
        lg = bank[:, 0, 0:B * E].rearrange("p (b e) -> p b e", b=B)

        def over_e(col):
            return r1[:, col, :].unsqueeze(2).broadcast_to([P, B, E])

        link(dve.tensor_reduce(r1[:, 0, :], lg, AX.X, ALU.max))
        dve.tensor_tensor(lgs[:, 0, :, :], lg, over_e(0), ALU.subtract).then_inc(log_sub, 1)

        def choose_experts():
            dve.wait_ge(log_exp, 1)
            link(dve.tensor_reduce(r1[:, 1, :], lgs[:, 1, :, :], AX.X, ALU.add))
            link(dve.reciprocal(r1[:, 2, :], r1[:, 1, :]))
            link(dve.tensor_tensor(lgs[:, 2, :, :], lgs[:, 1, :, :], over_e(2), ALU.mult))
            link(dve.tensor_tensor(lgs[:, 3, :, :], lgs[:, 2, :, :], gbias[:, :, :], ALU.add))
            for b in range(B):
                link(dve.max(top[:, b, :], lgs[:, 3, b, :]))
                link(dve.max_index(topi[:, b, :], top[:, b, :], lgs[:, 3, b, :]))
            link(dve.tensor_copy(topf[:, :, :], topi[:, :, :]))
            for b in range(B):
                link(dve.tensor_scalar(lgs[:, 4, b, :], iota[:, :], topf[:, b, 0:1], None, ALU.is_equal))
                link(dve.scalar_tensor_tensor(lgs[:, 5, b, :], iota[:, :], topf[:, b, 1:2], lgs[:, 4, b, :],
                                              ALU.is_equal, ALU.add))
            dve.scalar_tensor_tensor(lgs[:, 0, :, :], lgs[:, 5, :, :], 1.0 / WS, lgs[:, 2, :, :], ALU.mult, ALU.mult)\
                .then_inc(g_made, 1)

        choose_experts()

        dve.wait_ge(one_gate, 1)

        def unit(i, off, total):
            for it in range(C):
                n = it if (total and off == 0) else C * at(i, off) + it
                if it == 0 and not (total and off == 0):
                    dve.wait_ge(g_spread, 16)
                dve.wait_ge(sil_done, n + 1)
                dve.tensor_tensor(hf[:, it % 2, :], bank[:, 5 + 2 * (it % 2), :], sil[:, it % 2, :], ALU.mult)\
                    .then_inc(mul_done, 1)
                dve.wait_ge(mul_done, n + 1)
                dve.tensor_tensor(hf[:, it % 2, :], hf[:, it % 2, :], gate[:, at(i, off), :], ALU.mult)\
                    .then_inc(h_full, 1)
                dve.wait_ge(h_hi, n + 1)
                if not (total and off == 0 and it < 2):
                    dve.wait_ge(down_done, n - 1)
                dve.tensor_tensor(hl[:, it % 2, :], hf[:, it % 2, :], hh[:, it % 2, :], ALU.subtract)\
                    .then_inc(h_lo, 1)
                if it < 3 and exists(off, total, 1):
                    split_weights(i, off + 1, it)
                if total and off == 0 and it == 2:
                    dve.wait_ge(gT_ready, 1)
                    dve.tensor_copy(gT[:, :], bank[0:E, 4, :]).then_inc(gT_done, 1)

        run_units(dve, unit)
        for b in range(B):
            dve.wait_ge(y_ready, b + 1)
            dve.scalar_tensor_tensor(x1[:, b, :], bank[:, b, :], 1.0 / WS, x2[:, b, :], ALU.mult, ALU.add)\
                .then_inc(x3_done, 1)

    @blk.tensor
    def _(pe):
        def queries(i, off):
            pe.wait_ge(xs_step, 3 * at(i, off) + 3)
            if not (isinstance(at(i, off), int) and off == 0):
                pe.wait_ge(m_taken, MT * at(i, off) - 1)
            for a in range(HG):
                mm = pe.transpose(half_bank(4)[0:KS, a * P:(a + 1) * P], xs[:, off % 2, a, 0:KS], idh[:, :])
            mm.then_inc(m_ready, 1)

        def max_scores(i, off, k):
            a, q = block_of(k)
            if k == 1:
                pe.wait_ge(m_taken, MT * at(i, off) + 1)
            else:
                pe.wait_ge(m_taken, MT * at(i, off) + k - 1)
            if k % (2 * HG) == 1:
                pe.wait_ge(k_rep[off % 2][k // (2 * HG)], 16 * 6 * uses(i, off))
            pe.matmul(bank[:, 4 + k % 2, :], q1[:, a, :], kstk[0:KS, off % 2, a, q * 512:(q + 1) * 512],
                      start=True, stop=True).then_inc(m_ready, 1)

        def shifted(i, off):
            pe.wait_ge(mx_step, 3 * at(i, off) + 3)
            pe.wait_ge(m_taken, MT * at(i, off) + MT - 2)
            for a in range(HG):
                mm = pe.transpose(half_bank(5)[0:KM, a * P:(a + 1) * P], xs[:, off % 2, a, :], idh[:, :])
            mm.then_inc(m_ready, 1)

        def scores(i, off, hs, j):
            if hs == 0 and j == 0:
                pe.wait_ge(m_taken, MT * at(i, off) + MT)
            if j == 0 and not (isinstance(at(i, off), int) and off == 0 and hs < 2):
                pe.wait_ge(exp_done, HS * at(i, off) + hs - 1)
            tile = 2 * hs + j
            for a in range(HG):
                mm = pe.matmul(bank[:, 2 * (hs % 2) + j, a * P:(a + 1) * P],
                               kstk[:, off % 2, a, tile * P:(tile + 1) * P], q2[:, off % 2, a, :],
                               start=True, stop=True)
            if j == 1:
                mm.then_inc(st_done, 1)

        def values(i, off, hs, j):
            if j == 0:
                pe.wait_ge(exp_done, HS * at(i, off) + hs + 1)
            if hs == 0 and j == 0:
                pe.wait_ge(v_in[off % 2], 16 * uses(i, off))
                if not (isinstance(at(i, off), int) and off < 2):
                    pe.wait_ge(o_free, at(i, off - 1))
            tile = 2 * hs + j
            for a in range(HG):
                mm = pe.matmul(bank[a * HD:(a + 1) * HD, 6 + off % 2, 0:P], v[:, off % 2, tile, a * HD:(a + 1) * HD],
                               pt[:, hs % 4, j, a, :], start=(tile == 0), stop=(tile == J - 1),
                               skip_group_check=True)
            if j == 1:
                mm.then_inc(pv_done, 1)

        def denominators(i, off, hs):
            pe.wait_ge(add_done, HS * at(i, off) + hs + 1)
            for a in range(HG):
                mm = pe.matmul(bank[a * HD:(a + 1) * HD, 6 + off % 2, P:2 * P], ones[:, :], ps2[:, hs % 4, a, :],
                               start=False, stop=(hs == HS - 1), skip_group_check=True)
            mm.then_inc(den_done, 1)
            if hs == HS - 1:
                pe.wait_ge(den_done, HS * at(i, off) + HS)
                pe.nop().then_inc(o_ready, 1)

        pe.wait_ge(ones_set, 1)
        pe.wait_ge(id_in, 32)
        queries(0, 0)
        for k in range(1, MT - 1):
            max_scores(0, 0, k)
        shifted(0, 0)
        queries(0, 1)
        scores(0, 0, 0, 0)
        scores(0, 0, 0, 1)

        SPREAD = [(1, 2, 3), (4, 5, 6), (7, 8, 9), (10, 11, 12), (13, 14, 15), (16,)]

        def body(i, off, total):
            more = exists(off, total, 1)
            for hs in range(HS):
                tenants = list(SPREAD[hs]) if more and hs < len(SPREAD) else []

                def one_max():
                    if tenants:
                        max_scores(i, off + 1, tenants.pop(0))

                one_max()
                for j in range(2):
                    if hs + 1 < HS:
                        scores(i, off, hs + 1, j)
                    elif more:
                        scores(i, off + 1, 0, j)
                one_max()
                if hs == 7 and exists(off, total, 2):
                    queries(i, off + 2)
                if hs == 6 and more:
                    shifted(i, off + 1)
                values(i, off, hs, 0)
                values(i, off, hs, 1)
                one_max()
                if hs > 1:
                    denominators(i, off, hs - 2)
                elif not (total and off == 0):
                    denominators(i, off - 1, HS - 2 + hs)

        run_groups(pe, body)
        denominators(0, G - 1, HS - 2)
        denominators(0, G - 1, HS - 1)

        pe.wait_ge(consts, NC)
        pe.wait_ge(exp_done, HS * G)

        def project(b):
            pe.wait_ge(o_free, C * (b + 1))
            for c in range(C):
                mm = pe.matmul(bank[:, b, :], ao[:, C * b + c, :], wproj[:, c, :], start=(c == 0), stop=(c == C - 1))
            mm.then_inc(proj_done, 1)

        def transpose_normed(b):
            pe.wait_ge(hn_done, b + 1)
            for c in range(C):
                mm = pe.transpose(bank[:, 4 + b, c * P:(c + 1) * P], hn[:, b, c * P:(c + 1) * P], idf[:, :])
            mm.then_inc(hnT_ready, 1)

        def scan_in(b0, b1, n, columns, ready):
            pe.wait_ge(hnT_act, b1)
            part = slice(b0 * P, b1 * P)
            for c in range(C):
                mm = pe.matmul(bank[:, n, part], win[:, c, columns], hnT[:, c, part], start=(c == 0),
                               stop=(c == C - 1))
            mm.then_inc(ready, 1)

        UZ, GG = slice(0, 2 * ST), slice(2 * ST, 4 * ST)
        project(0)
        project(1)
        transpose_normed(0)
        project(2)
        transpose_normed(1)
        project(3)
        transpose_normed(2)
        pe.wait_ge(win_done, C)
        pe.wait_ge(x1_done, 1)
        scan_in(0, 2, 0, UZ, uz_ready)
        pe.wait_ge(x1_done, 2)
        scan_in(0, 1, 1, GG, g_ready)
        transpose_normed(3)
        scan_in(1, 2, 1, GG, g_ready)
        scan_in(2, B, 0, UZ, uz_ready)

        pe.wait_ge(x1_done, B)
        pe.wait_ge(uz_done, 1)
        pe.matmul(bank[:, 2, :], wx[ST:2 * ST, :], uz[ST:2 * ST, :], start=True, stop=True).then_inc(dt_ready, 1)
        pe.matmul(bank[:, 3, :], wx[0:ST, :], uz[0:ST, :], start=True, stop=True).then_inc(ut_ready, 1)
        scan_in(2, B, 1, GG, g_ready)
        pe.wait_ge(wo_lo, 1)
        for b in range(B):
            pe.wait_ge(y_done, b // 2 + 1)
            for n in range(2):
                mm = pe.matmul(bank[:, 4 + b, :], yst[:, b * P:(b + 1) * P], wo[:, n, :], start=(n == 0), stop=(n == 1))
            mm.then_inc(scan_out, 1)

        def up(q, it, tokens=slice(0, T), last=True):
            part = slice(it * P, (it + 1) * P)
            for m in range(2):
                for c in range(C):
                    o = bank[:, 4 + 2 * (it % 2) + m, tokens]
                    pe.matmul(o, ws[:, q, 0, m, c, part], xh[:, c, tokens], start=(c == 0), stop=False)
                    pe.matmul(o, ws[:, q, 0, m, c, part], xl[:, c, tokens], start=False, stop=False)
                    mm = pe.matmul(o, ws[:, q, 1, m, c, part], xh[:, c, tokens], start=False, stop=(c == C - 1))
            if last:
                mm.then_inc(ab_ready, 1)

        def transpose_tokens(b):
            pe.wait_ge(h3_done, b + 1)
            for c in range(C):
                mm = pe.transpose(bank[:, b, c * P:(c + 1) * P], xn[:, b, c * P:(c + 1) * P], idf[:, :])
            mm.then_inc(h3T_ready, 1)

        FIRST, SECOND = slice(0, T // 2), slice(T // 2, T)
        for b in range(B):
            transpose_tokens(b)
        pe.wait_ge(w_hi, 2)
        pe.wait_ge(w_lo, 2)
        pe.wait_ge(xl_done, 2)
        pe.wait_ge(x2_done, B)
        up(0, 0, FIRST, False)
        pe.wait_ge(gw_split, 1)
        for b in range(B):
            part = slice(b * P, (b + 1) * P)
            pe.wait_ge(xl_done, b + 1)
            o = bank[:, 0, b * E:(b + 1) * E]
            for c in range(C):
                pe.matmul(o, xh[:, c, part], gwh[:, c, 0:E], start=(c == 0), stop=False)
                pe.matmul(o, xh[:, c, part], gwh[:, c, E:2 * E], start=False, stop=False)
                mm = pe.matmul(o, xl[:, c, part], gwh[:, c, 0:E], start=False, stop=(c == C - 1))
        mm.then_inc(log_ready, 1)
        up(0, 1, FIRST, False)
        up(0, 0, SECOND)
        up(0, 1, SECOND)
        pe.wait_ge(zero_set, 1)
        pe.wait_ge(log_sub, 1)
        for b in range(B):
            pe.matmul(bank[:, b, :], zero[:, 0:P], zero[:, :], start=True, stop=False, skip_group_check=True)

        def down(q, it, n, each=None):
            pe.wait_ge(h_hi, n)
            pe.wait_ge(h_lo, n)
            for b in range(B):
                part = slice(b * P, (b + 1) * P)
                pe.matmul(bank[:, b, :], hh[:, it % 2, part], ws[:, q, 0, 2, it, :], start=False, stop=False,
                          skip_group_check=True)
                pe.matmul(bank[:, b, :], hh[:, it % 2, part], ws[:, q, 1, 2, it, :], start=False, stop=False,
                          skip_group_check=True)
                mm = pe.matmul(bank[:, b, :], hl[:, it % 2, part], ws[:, q, 0, 2, it, :], start=False,
                               stop=bool(each), skip_group_check=True)
                if each:
                    mm.then_inc(each, 1)
            if not each:
                mm.then_inc(down_done, 1)

        def unit(i, off, total):
            first = total and off == 0
            for it in range(C):
                n = it if first else C * at(i, off) + it
                if it == 0 and not first:
                    pe.wait_ge(w_hi, 3 * at(i, off) + 2)
                    pe.wait_ge(w_lo, 3 * at(i, off) + 2)
                if not (first and it < 2):
                    pe.wait_ge(mul_done, n - 1)
                if not (first and it < 2):
                    up(off % 2, it)
                if first and it == C - 1:
                    pe.wait_ge(g_made, 1)
                    pe.wait_ge(mul_done, C - 1)
                    for b in range(B):
                        mm = pe.transpose(bank[0:E, 4, b * P:(b + 1) * P], lgs[:, 0, b, :], idf[:, :])
                    mm.then_inc(gT_ready, 1)
                if it == 0:
                    if not first:
                        down((off - 1) % 2, C - 1, n)
                else:
                    if it == 1:
                        pe.wait_ge(w_hi, 3 * at(i, off) + 3)
                        pe.wait_ge(w_lo, 3 * at(i, off) + 3)
                    down(off % 2, it - 1, n)
                if first and it == C - 1:
                    pe.wait_ge(gT_done, 1)

        run_units(pe, unit)
        down((U - 1) % 2, C - 1, C * U, y_ready)

    block.__exit__(None, None, None)


def kernel(**inputs):
    import concourse.bacc as bacc
    from concourse.bass_utils import run_bass_kernel_spmd

    a = {k.replace("L0_", ""): np.asarray(v) for k, v in inputs.items()}
    ctx = a["ctx_1024"]
    def rows(w):
        w = w.reshape(*w.shape[:-2], w.shape[-2] // P, P, w.shape[-1])
        return np.moveaxis(w, -2, -3)

    def spread(row):
        return np.broadcast_to(row, (P, *row.shape))

    w1 = np.concatenate([a["ffn_sw1"].reshape(2, D, D), a["ffn_w1"]])
    w3 = np.concatenate([a["ffn_sw3"].reshape(2, D, D), a["ffn_w3"]])
    w2 = np.concatenate([a["ffn_sw2"].reshape(D, 2, D).transpose(1, 0, 2), a["ffn_w2"]])
    ffw = np.stack([rows(w.transpose(0, 2, 1)) for w in (w1, w3, w2)], axis=1)
    cols = np.zeros((P, 4), np.float32)
    cols[:, 0] = a["attn_b_in"][:P]
    for n, part in enumerate((a["attn_b_in"][P:], a["attn_b_x"], a["attn_b_dt"])):
        cols[:, n + 1] = np.concatenate([part, part])
    w_in = a["attn_W_in"]
    w_x = np.concatenate([a["attn_W_x"], a["attn_W_dt"]])
    arrays = {
        "x": a["x"].transpose(1, 0, 2),
        "keysT": ctx.reshape(B, 4, S // 4, C, HG, HD).transpose(0, 3, 1, 5, 4, 2).reshape(G, P, HG, S // 4),
        "vals": ctx.reshape(B, J, P, C, P).transpose(0, 3, 2, 1, 4).reshape(G, P, J, P),
        "ffw": ffw,
        "wproj": rows(a["xattn_w_proj"].T),
        "win": rows(np.concatenate([w_in, w_in[:, 2 * ST:]], axis=1)),
        "normw": a["attn_norm_w"].reshape(C, P).T,
        "bproj": spread(a["xattn_b_proj"]),
        "bout": spread(a["attn_b_out"]),
        "wx": np.concatenate([w_x, w_x], axis=1),
        "wout": np.concatenate([a["attn_W_out"], a["attn_W_out"]]),
        "cols": cols,
        "gwt": rows(a["ffn_gate_w"].T),
        "gbias": spread(np.broadcast_to(a["ffn_gate_bias"], (B, E))),
        "iota": spread(np.arange(E, dtype=np.float32)),
        "idf": np.eye(P, dtype=np.float32),
        "idh": np.eye(P, dtype=np.float16),
        "ones": np.ones((KM - KS, 2, HG, S), np.float16),
    }
    nc = bacc.Bacc("TRN2", target_bir_lowering=False, num_devices=1)
    feed, aps = {}, {}
    for name, arr in arrays.items():
        arr = np.ascontiguousarray(arr)
        feed[f"in_{name}"] = arr
        aps[name] = nc.dram_tensor(f"in_{name}", arr.shape, mybir.dt.from_np(arr.dtype), kind="ExternalInput").ap()
    out = nc.dram_tensor("out_0", (B, P, D), F32, kind="ExternalOutput").ap()
    build_program(nc, aps, out)
    r = run_bass_kernel_spmd(nc, [feed], core_ids=[0])
    return r.results[0]["out_0"]
```
